# Optimizing a Trainium2 kernel written in Bass

```python
import numpy as np
import jax
import jax.numpy as jnp

def _softmax(x, axis=-1):
    return jax.nn.softmax(x, axis=axis)

def _gelu(x):
    return jax.nn.gelu(x, approximate=True)

def _silu(x):
    return jax.nn.silu(x)

def _sigmoid(x):
    return jax.nn.sigmoid(x)

def _layernorm(x, axis=-1, eps=1e-05):
    m = jnp.mean(x, axis=axis, keepdims=True)
    v = jnp.var(x, axis=axis, keepdims=True)
    return (x - m) / jnp.sqrt(v + eps)

def _scatter_add(tgt, idx, src, axis=0):
    return tgt.at[idx].add(src)

def _segment_sum(src, seg, n):
    return jax.ops.segment_sum(src, seg, n)
kernel_name = 'mk_gnn_resnorm_d2_gnn_r32_d59480'

def setup_inputs(seed: int=0):
    np.random.seed(seed)
    _w = jnp.asarray

    def _rec_inputs():
        import jax
        import jax.numpy as jnp
        _gk = jax.random.key(seed)
        x = -0.000202 + 1 * jax.random.normal(jax.random.fold_in(_gk, 1), (3125, 128), jnp.float32)
        src = jax.random.randint(jax.random.fold_in(_gk, 2), (100000,), 0, 3125, jnp.int32)
        dst = jax.random.randint(jax.random.fold_in(_gk, 3), (100000,), 0, 3125, jnp.int32)
        _o = jnp.argsort(dst, stable=True)
        src = src[_o]
        dst = dst[_o]
        edge_type_8 = jax.random.randint(jax.random.fold_in(_gk, 12), (100000,), 0, 8, jnp.int32)
        return (x, src, dst, edge_type_8)
    x, src, dst, edge_type_8 = _rec_inputs()

    def _L0_gnn_setup():
        import jax, jax.numpy as jnp
        import numpy as np
        N = 50000
        E = 25000
        DIN, DH, DOUT, DCTX = (128, 128, 128, 64)

        def gcn_conv(x, src, dst, W, b):
            n = x.shape[0]
            h = x @ W
            loop = jnp.arange(n, dtype=src.dtype)
            s = jnp.concatenate([src, loop])
            d = jnp.concatenate([dst, loop])
            deg = jax.ops.segment_sum(jnp.ones(s.shape, h.dtype), d, num_segments=n)
            dinv = jax.lax.rsqrt(jnp.maximum(deg, 1.0))
            norm = dinv[s] * dinv[d]
            msgs = h[s] * norm[:, None]
            return jax.ops.segment_sum(msgs, d, num_segments=n) + b
        key = jax.random.key(seed)
        ks = jax.random.split(key, 8)
        x = jax.random.normal(ks[0], (N, DIN), jnp.float32)
        edge_index = jax.random.randint(ks[1], (2, E), 0, N, dtype=jnp.int64)
        ctx = jax.random.normal(ks[2], (1, DCTX), jnp.float32)
        init = lambda k, shp, fan: jax.random.normal(k, shp, jnp.float32) / np.sqrt(fan).astype(np.float32)
        W1 = init(ks[3], (DIN, DH), DIN)
        b1 = jnp.zeros((DH,), jnp.float32)
        W2 = init(ks[4], (DH, DOUT), DH)
        b2 = jnp.zeros((DOUT,), jnp.float32)
        Wg = init(ks[5], (DCTX, DOUT), DCTX)
        bg = jnp.zeros((DOUT,), jnp.float32)
        Wb = init(ks[6], (DCTX, DOUT), DCTX)
        return {'x': x, 'ctx': ctx, 'W1': W1, 'b1': b1, 'W2': W2, 'b2': b2, 'Wg': Wg, 'bg': bg, 'Wb': Wb, 'edge_index': edge_index}
    _L0_gnn_all = _L0_gnn_setup()
    _L0_gnn_in = {k: v for k, v in _L0_gnn_all.items() if k in ('ctx', 'W1', 'b1', 'W2', 'b2', 'Wg', 'bg', 'Wb')}
    del _L0_gnn_all

    def _L1_gnn_setup():
        import jax, jax.numpy as jnp
        import numpy as np
        N_ENT = 3125

        def _rgcn_layer(x, W, SW, b, src, dst, rel):
            xt = jnp.einsum('nd,rde->rne', x, W)
            msg = xt[rel, src]
            agg = jax.ops.segment_sum(msg, dst, num_segments=x.shape[0])
            return jax.nn.relu(agg + x @ SW + b)
        key = jax.random.key(seed)
        ks = jax.random.split(key, 8)
        d, R, E = (128, 8, 18750)
        scale = 1.0 / np.sqrt(d)
        return {'entity_emb': jax.random.normal(ks[0], (N_ENT, d), dtype=jnp.float32), 'w1': jax.random.normal(ks[1], (R, d, d), dtype=jnp.float32) * scale, 'sl1': jax.random.normal(ks[2], (d, d), dtype=jnp.float32) * scale, 'b1': jnp.zeros((d,), dtype=jnp.float32), 'w2': jax.random.normal(ks[3], (R, d, d), dtype=jnp.float32) * scale, 'sl2': jax.random.normal(ks[4], (d, d), dtype=jnp.float32) * scale, 'b2': jnp.zeros((d,), dtype=jnp.float32), 'edge_index': jax.random.randint(ks[5], (2, E), 0, N_ENT, dtype=jnp.int64), 'edge_type': jax.random.randint(ks[6], (E,), 0, R, dtype=jnp.int64)}
    _L1_gnn_all = _L1_gnn_setup()
    _L1_gnn_in = {k: v for k, v in _L1_gnn_all.items() if k in ('w1', 'sl1', 'b1', 'w2', 'sl2', 'b2')}
    del _L1_gnn_all
    return {'x': x, 'src': src, 'dst': dst, 'edge_type_8': edge_type_8, 'L0_gnn_ctx': _L0_gnn_in['ctx'], 'L0_gnn_W1': _L0_gnn_in['W1'], 'L0_gnn_b1': _L0_gnn_in['b1'], 'L0_gnn_W2': _L0_gnn_in['W2'], 'L0_gnn_b2': _L0_gnn_in['b2'], 'L0_gnn_Wg': _L0_gnn_in['Wg'], 'L0_gnn_bg': _L0_gnn_in['bg'], 'L0_gnn_Wb': _L0_gnn_in['Wb'], 'L1_gnn_w1': _L1_gnn_in['w1'], 'L1_gnn_sl1': _L1_gnn_in['sl1'], 'L1_gnn_b1': _L1_gnn_in['b1'], 'L1_gnn_w2': _L1_gnn_in['w2'], 'L1_gnn_sl2': _L1_gnn_in['sl2'], 'L1_gnn_b2': _L1_gnn_in['b2']}

def reference(x, src, dst, edge_type_8, L0_gnn_ctx, L0_gnn_W1, L0_gnn_b1, L0_gnn_W2, L0_gnn_b2, L0_gnn_Wg, L0_gnn_bg, L0_gnn_Wb, L1_gnn_w1, L1_gnn_sl1, L1_gnn_b1, L1_gnn_w2, L1_gnn_sl2, L1_gnn_b2):
    import jax
    import jax.numpy as jnp

    def _L0_gnn_ref(x, ctx, W1, b1, W2, b2, Wg, bg, Wb, edge_index):
        import jax, jax.numpy as jnp
        import numpy as np
        N = 50000
        E = 25000
        DIN, DH, DOUT, DCTX = (128, 128, 128, 64)

        def gcn_conv(x, src, dst, W, b):
            n = x.shape[0]
            h = x @ W
            loop = jnp.arange(n, dtype=src.dtype)
            s = jnp.concatenate([src, loop])
            d = jnp.concatenate([dst, loop])
            deg = jax.ops.segment_sum(jnp.ones(s.shape, h.dtype), d, num_segments=n)
            dinv = jax.lax.rsqrt(jnp.maximum(deg, 1.0))
            norm = dinv[s] * dinv[d]
            msgs = h[s] * norm[:, None]
            return jax.ops.segment_sum(msgs, d, num_segments=n) + b
        src, dst = (edge_index[0], edge_index[1])
        gate = jax.nn.sigmoid(ctx @ Wg + bg)
        bias = ctx @ Wb
        h = jax.nn.leaky_relu(gcn_conv(x, src, dst, W1, b1), negative_slope=0.2)
        out = gcn_conv(h, src, dst, W2, b2)
        return out * gate + bias

    def _L1_gnn_ref(entity_emb, w1, sl1, b1, w2, sl2, b2, edge_index, edge_type):
        import jax, jax.numpy as jnp
        import numpy as np
        N_ENT = 3125

        def _rgcn_layer(x, W, SW, b, src, dst, rel):
            xt = jnp.einsum('nd,rde->rne', x, W)
            msg = xt[rel, src]
            agg = jax.ops.segment_sum(msg, dst, num_segments=x.shape[0])
            return jax.nn.relu(agg + x @ SW + b)
        src, dst = (edge_index[0], edge_index[1])
        x = _rgcn_layer(entity_emb, w1, sl1, b1, src, dst, edge_type)
        x = _rgcn_layer(x, w2, sl2, b2, src, dst, edge_type)
        return x
    edge_index = jnp.stack([src, dst])
    x = _layernorm(x + _L0_gnn_ref(x, L0_gnn_ctx, L0_gnn_W1, L0_gnn_b1, L0_gnn_W2, L0_gnn_b2, L0_gnn_Wg, L0_gnn_bg, L0_gnn_Wb, edge_index), axis=-1)
    x = _layernorm(x + _L1_gnn_ref(x, L1_gnn_w1, L1_gnn_sl1, L1_gnn_b1, L1_gnn_w2, L1_gnn_sl2, L1_gnn_b2, edge_index, edge_type_8), axis=-1)
    return x

_drawn_inputs = setup_inputs


def setup_inputs(seed=0):
    import zlib

    import numpy as np

    out = dict(_drawn_inputs(seed))
    spreads = {'L0_gnn_b1': (0.0, 0.287),
     'L0_gnn_b2': (0.0, 0.1),
     'L0_gnn_bg': (0.0, 0.8),
     'L1_gnn_b1': (0.0, 0.708),
     'L1_gnn_b2': (0.0, 2.0)}
    factors = {'L0_gnn_W1': 8.0, 'L0_gnn_Wg': 3.507}
    for name, (base, spread) in spreads.items():
        noise = np.random.default_rng([zlib.crc32(name.encode()), seed]).standard_normal(out[name].shape)
        drawn = base * np.exp(spread * noise) if base else spread * noise
        out[name] = jnp.asarray(drawn.astype(out[name].dtype))
    for name, factor in factors.items():
        out[name] = (out[name] * factor).astype(out[name].dtype)
    return out
```

```python
import concourse.bass as bass
from concourse import mybir
from contextlib import ExitStack

N_NODES, D, R, CTX = 3125, 128, 8, 64
E = 100000
P = 128
TILES = -(-N_NODES // P)
NP = TILES * P
LAST = N_NODES - (TILES - 1) * P
BATCH = 1024
CH = BATCH // P
NB = -(-E // BATCH)
TAIL = E - (NB - 1) * BATCH
W = 64
PASSES = NP // W
NO_NODE = 8191
LN_EPS = 1e-5
SLOPE = 0.2
BANK = 512
STAGES = 8
TBANKS = 6
WIN_BANK = 6
assert NB % 2 == 0 and NP % W == 0 and N_NODES + W <= NP + W


def groups_of(layer):
    tables = -(-TILES // 4) if layer < 2 else 2 * TILES
    return [("table", k) for k in range(tables)] + [("self", k) for k in range(-(-NP // BANK))]


def gnn_kernel(nc, x, src, dst, rel, ctx_in, W1, b1, W2, b2, Wg, bg, Wb, w1, sl1, rb1, w2, sl2, rb2, out):
    f32, i32 = mybir.dt.float32, mybir.dt.int32
    ALU, ACT, AX = mybir.AluOpType, mybir.ActivationFunctionType, mybir.AxisListType

    table_gcn = nc.dram_tensor("table_gcn", (NP, D), f32).ap()
    table_rel = nc.dram_tensor("table_rel", (NP * R, D), f32).ap()

    with ExitStack() as stack:
        def sb(name, shape, dt=f32):
            return stack.enter_context(nc.sbuf_tensor(name, shape, dt))

        def sem(name):
            return stack.enter_context(nc.semaphore(name))

        dst_i, src_i, rel_i = (sb(n, [NB, BATCH], i32) for n in ("dst_i", "src_i", "rel_i"))
        dst_f, src_f, row_f = (sb(n, [NB, BATCH]) for n in ("dst_f", "src_f", "row_f"))
        inside = sb("inside", [NB, BATCH])
        inside_n = sb("inside_n", [NB, 1])
        dst_t, src_t, row_t = (sb(n, [P, CH, NB]) for n in ("dst_t", "src_t", "row_t"))
        base_i = sb("base_i", [1, NB], i32)
        flag_i = sb("flag_i", [1, 1], i32)
        ident = sb("ident", [P, P])
        ones = sb("ones", [P, P])
        node_id = sb("node_id", [P, NP])
        xn = sb("xn", [P, TILES, D])
        xT = sb("xT", [P, NP])
        tin = sb("tin", [P, NP])
        acc = sb("acc", [P, NP])
        dinv = sb("dinv", [P, NP])
        onehot = sb("onehot", [P, 2, CH, W])
        msgs = sb("msgs", [P, 2, CH, D])
        idx = sb("idx", [P, 2, CH], i32)
        stage = sb("stage", [P, STAGES, BANK])
        wg1, wg2, ws1, ws2 = (sb(n, [P, D]) for n in ("wg1", "wg2", "ws1", "ws2"))
        wr1, wr2 = (sb(n, [P, R, D]) for n in ("wr1", "wr2"))
        wgate, wbias = (sb(n, [CTX, D]) for n in ("wgate", "wbias"))
        cols = sb("cols", [P, 5])
        ctx_c = sb("ctx_c", [CTX, 1])
        gate = sb("gate", [P, 1])
        shift = sb("shift", [P, 1])
        eps = sb("eps", [P, 1])
        stats = sb("stats", [P, TILES, 6])
        mv = sb("mv", [P, TILES, 2])
        std = sb("std", [P, TILES])
        rstd = sb("rstd", [P, TILES])
        ps = stack.enter_context(nc.psum_tensor("ps", [P, 8, BANK], f32))

        edges_loaded, x_loaded, weights_loaded = sem("edges_loaded"), sem("x_loaded"), sem("weights_loaded")
        edges_cleared, x_cleared = sem("edges_cleared"), sem("x_cleared")
        ident_ready, node_id_ready = sem("ident_ready"), sem("node_id_ready")
        dve_step, act_step, pool_step = sem("dve_step"), sem("act_step"), sem("pool_step")
        edges_float = sem("edges_float")
        edges_turned = sem("edges_turned")
        counted = sem("counted")
        mode_ready = sem("mode_ready")
        x_turned = sem("x_turned")
        x_copied = sem("x_copied")
        gate_product, gate_ready = sem("gate_product"), sem("gate_ready")
        onehot_ready, window_ready, window_free = sem("onehot_ready"), sem("window_ready"), sem("window_free")
        idx_ready = sem("idx_ready")
        gathered = [sem(f"gathered{u}") for u in range(2)]
        deg_ready, deg_sqrt = sem("deg_ready"), sem("deg_sqrt")
        tin_ready = sem("tin_ready")
        product_done, dve_evac, act_evac = sem("product_done"), sem("dve_evac"), sem("act_evac")
        stored = [sem(f"stored{u}") for u in range(STAGES)]
        y_ready, y_turned, var_ready, std_ready = sem("y_ready"), sem("y_turned"), sem("var_ready"), sem("std_ready")
        normed, xn_turned = sem("normed"), sem("xn_turned")
        out_stored = sem("out_stored")

        SETUP_TURNS = 6
        XG = -(-TILES // 4)
        WEIGHT_LOADS = 15
        layer_in = [tin, tin, xT, tin]
        layer_w = [wg1, wg2, wr1, wr2]
        layer_self = [wg1, wg2, ws1, ws2]

        plan, g0, q0 = [], 0, 0
        for layer in range(4):
            rows = []
            for kind, k in groups_of(layer):
                rows.append((g0, kind, k, q0 if kind == "table" else None))
                g0 += 1
                q0 += kind == "table"
            plan.append(rows)

        def evacuated(g):
            return (act_evac if g % 2 else dve_evac), g // 2 + 1

        def table_view(layer, k):
            if layer < 2:
                n = min(4, TILES - 4 * k)
                return table_gcn.rearrange("(t p) f -> p t f", p=P)[:, 4 * k:4 * k + n, :], n * D
            t, h = k // 2, k % 2
            return table_rel.rearrange("(t p r) f -> p t (r f)", p=P, r=R)[:, t, h * BANK:(h + 1) * BANK], BANK

        def passes(eng, slow, body):
            if slow:
                with eng.Fori(0, PASSES) as p:
                    with eng.Fori(0, NB // 2) as k:
                        body(k, p * NB, p * W)
            else:
                with eng.Fori(0, NB // 2) as k:
                    body(k, 0, None)

        def per_loop(slow):
            return NB * (PASSES if slow else 1)

        block = stack.enter_context(nc.Block())

        @block.sync
        def _(sp):
            sp.wait_ge(edges_cleared, 3)
            for dram, tile in ((dst, dst_i), (src, src_i), (rel, rel_i)):
                full = 96
                sp.dma_start(tile[0:full, :], dram[0:full * BATCH].rearrange("(b e) -> b e", e=BATCH)).then_inc(edges_loaded, 16)
                sp.dma_start(tile[full:NB - 1, :], dram[full * BATCH:(NB - 1) * BATCH].rearrange("(b e) -> b e", e=BATCH)).then_inc(edges_loaded, 16)
                sp.dma_start(tile[NB - 1:NB, 0:TAIL], dram[(NB - 1) * BATCH:E].rearrange("(b e) -> b e", b=1)).then_inc(edges_loaded, 16)
            for tile, dram in ((wg1, W1), (wg2, W2), (ws1, sl1), (ws2, sl2), (wgate, Wg), (wbias, Wb)):
                sp.dma_start(tile[:, :], dram).then_inc(weights_loaded, 16)
            for tile, dram in ((wr1, w1), (wr2, w2)):
                sp.dma_start(tile[:, :, :], dram.rearrange("r d e -> d r e")).then_inc(weights_loaded, 16)
            for c, dram in enumerate((b1, b2, bg, rb1, rb2)):
                sp.dma_start(cols[:, c:c + 1], dram.rearrange("(p a) -> p a", a=1)).then_inc(weights_loaded, 16)
            sp.dma_start(ctx_c[:, :], ctx_in.rearrange("a c -> c a")).then_inc(weights_loaded, 16)
            sp.dma_start(cols[:, 0:1], b1.rearrange("(p a) -> p a", a=1)).then_inc(weights_loaded, 16) if WEIGHT_LOADS == 16 else None

            def rest(slow):
                for layer in range(4):
                    for g, kind, k, q in plan[layer]:
                        if kind != "table":
                            continue
                        view, n = table_view(layer, k)
                        sp.wait_ge(*evacuated(g))
                        src_ap = stage[:, q % STAGES, 0:n]
                        if layer < 2:
                            src_ap = src_ap.rearrange("p (t f) -> p t f", f=D)
                        sp.dma_start(view, src_ap).then_inc(stored[q % STAGES], 16)
                sp.wait_ge(normed, 2 * TILES)
                sp.dma_start(out[0:(TILES - 1) * P, :].rearrange("(t p) f -> p t f", p=P), xn[:, 0:TILES - 1, :]).then_inc(out_stored, 16)
                sp.dma_start(out[(TILES - 1) * P:N_NODES, :], xn[0:LAST, TILES - 1, :]).then_inc(out_stored, 16)
                sp.wait_ge(out_stored, 32)

            sp.wait_ge(mode_ready, 1)
            fast = sp.value_load(flag_i[0:1, 0:1], min_val=0, max_val=1)
            with sp.If(fast):
                rest(False)
            with sp.Else():
                rest(True)

        @block.gpsimd
        def _(pool):
            for tile, pad in ((dst_i, NO_NODE), (src_i, 0), (rel_i, 0)):
                nc.gpsimd.memset(tile[:, :], pad).then_inc(edges_cleared, 1)
            nc.gpsimd.memset(ident[:, :], 0.0).then_inc(pool_step, 1)
            pool.wait_ge(pool_step, 1)
            nc.gpsimd.affine_select(out=ident[:, :], in_=ident[:, :], compare_op=ALU.not_equal, fill=1.0, base=0,
                                    pattern=[[-1, P]], channel_multiplier=1).then_inc(ident_ready, 1)
            nc.gpsimd.iota(node_id[:, :], pattern=[[1, NP]], base=0, channel_multiplier=0,
                           allow_small_or_imprecise_dtypes=True).then_inc(node_id_ready, 1)

            def rest(slow):
                n_loop = per_loop(slow)
                for layer in range(4):
                    table = table_gcn if layer < 2 else table_rel
                    last_q = plan[layer][-1][0]
                    total = max(q for _, _, _, q in plan[layer] if q is not None) + 1
                    for s in range(STAGES):
                        pool.wait_ge(stored[s], 16 * len(range(s, total, STAGES)))

                    def body(k, before, base):
                        for u in range(2):
                            n = before + 2 * k + u + layer * n_loop
                            pool.wait_ge(idx_ready, n + 1)
                            pool.nop(nofuse=True)
                            for j in range(CH):
                                nc.gpsimd.indirect_dma_start(
                                    msgs[:, u, j, :], None, table,
                                    bass.IndirectOffsetOnAxis(ap=idx[:, u, j:j + 1], axis=0)).then_inc(gathered[u], 16)
                    passes(pool, slow, body)

            pool.wait_ge(mode_ready, 1)
            fast = pool.value_load(flag_i[0:1, 0:1], min_val=0, max_val=1)
            with pool.If(fast):
                rest(False)
            with pool.Else():
                rest(True)

        @block.scalar
        def _(act):
            act.wait_ge(x_cleared, 1)
            act.dma_start(xn[:, 0:TILES - 1, :], x[0:(TILES - 1) * P, :].rearrange("(t p) f -> p t f", p=P)).then_inc(x_loaded, 16)
            act.dma_start(xn[0:LAST, TILES - 1, :], x[(TILES - 1) * P:N_NODES, :]).then_inc(x_loaded, 16)
            for g in range(XG):
                n = min(4, TILES - 4 * g) * P
                act.wait_ge(x_turned, g + 1)
                nc.scalar.activation(xT[:, g * BANK:g * BANK + n], ps[:, g, 0:n], ACT.Copy).then_inc(x_copied, 1)
            act.wait_ge(gate_product, 1)
            nc.scalar.activation(gate[:, :], ps[:, 7, 0:1], ACT.Sigmoid, bias=cols[:, 2:3]).then_inc(gate_ready, 1)

            def rest(slow):
                n_loop = per_loop(slow)
                act.wait_ge(deg_ready, 1)
                nc.scalar.activation(dinv[:, :], dinv[:, :], ACT.Sqrt).then_inc(deg_sqrt, 1)
                for layer in range(4):
                    for g, kind, k, q in plan[layer]:
                        if g % 2 == 0:
                            continue
                        act.wait_ge(product_done, g + 1)
                        if kind == "table":
                            n = table_view(layer, k)[1]
                            if q >= STAGES:
                                act.wait_ge(stored[q % STAGES], 16 * (q // STAGES))
                            nc.scalar.activation(stage[:, q % STAGES, 0:n], ps[:, g % TBANKS, 0:n], ACT.Copy).then_inc(act_evac, 1)
                        else:
                            n = min(BANK, NP - k * BANK)
                            dstp = acc[:, k * BANK:k * BANK + n]
                            if layer < 2:
                                nc.scalar.activation(dstp, ps[:, g % TBANKS, 0:n], ACT.Copy).then_inc(act_evac, 1)
                            else:
                                nc.scalar.activation(dstp, ps[:, g % TBANKS, 0:n], ACT.Identity,
                                                     bias=cols[:, 1 + layer:2 + layer]).then_inc(act_evac, 1)
                    rows = src_t if layer < 2 else row_t

                    def body(k, before, base):
                        for u in range(2):
                            n = before + 2 * k + u + (layer + 1) * n_loop
                            act.wait_ge(window_ready, n - 1)
                            nc.scalar.activation(idx[:, u, :], rows[:, :, bass.ds(2 * k + u, 1)].rearrange("p c a -> p (c a)"),
                                                 ACT.Copy).then_inc(idx_ready, 1)
                    passes(act, slow, body)
                    if layer % 2:
                        ln = layer // 2
                        act.wait_ge(var_ready, ln + 1)
                        nc.scalar.activation(std[:, :], mv[:, :, 1], ACT.Sqrt, bias=eps[:, 0:1]).then_inc(std_ready, 1)

            act.wait_ge(mode_ready, 1)
            fast = act.value_load(flag_i[0:1, 0:1], min_val=0, max_val=1)
            with act.If(fast):
                rest(False)
            with act.Else():
                rest(True)

        @block.tensor
        def _(pe):
            pe.wait_ge(ident_ready, 1)
            pe.wait_ge(edges_float, 3)
            for a, tile in enumerate((dst_f, src_f, row_f)):
                for h in range(2):
                    for j in range(4):
                        c = 4 * h + j
                        last = nc.tensor.transpose(ps[:, 2 * a + h, j * NB:(j + 1) * NB], tile[:, c * P:(c + 1) * P], ident[0:NB, 0:NB])
                    last.then_inc(edges_turned, 1)
            nc.tensor.matmul(ps[0:1, 6, 0:NB], dst_f[:, 0:1], ident[0:NB, 0:NB], start=True, stop=True).then_inc(counted, 1)
            pe.wait_ge(edges_float, 4)
            nc.tensor.matmul(ps[0:1, 7, 0:1], inside_n[:, 0:1], ones[0:NB, 0:1], start=True, stop=True).then_inc(counted, 1)
            pe.wait_ge(mode_ready, 1)
            pe.wait_ge(x_loaded, 32)
            for t in range(TILES):
                last = nc.tensor.transpose(ps[:, t // 4, (t % 4) * P:(t % 4 + 1) * P], xn[:, t, :], ident[:, :])
                if t % 4 == 3 or t == TILES - 1:
                    last.then_inc(x_turned, 1)
            pe.wait_ge(weights_loaded, 16 * (WEIGHT_LOADS - 1))
            nc.tensor.matmul(ps[:, 7, 0:1], wgate[:, :], ctx_c[:, :], start=True, stop=True)
            nc.tensor.matmul(ps[:, 7, 1:2], wbias[:, :], ctx_c[:, :], start=True, stop=True).then_inc(gate_product, 1)
            pe.wait_ge(gate_ready, 2)

            def rest(slow):
                n_loop = per_loop(slow)

                def windows(loop):
                    def body(k, before, base):
                        for u in range(2):
                            n = before + 2 * k + u + loop * n_loop
                            pe.wait_ge(window_free, n + 1)
                            pe.wait_ge(onehot_ready, n + 1)
                            if loop:
                                pe.wait_ge(gathered[u], (before // 2 + k + (loop - 1) * (n_loop // 2) + 1) * (16 * CH) if not slow
                                           else (base * (NB // 2 * 16 * CH // W) + k * (16 * CH) + ((loop - 1) * (n_loop // 2) + 1) * 16 * CH))
                            for j in range(CH):
                                left = msgs[:, u, j, :] if loop else ones[:, :]
                                last = nc.tensor.matmul(ps[:, WIN_BANK + u, 0:W], left, onehot[:, u, j, :],
                                                        start=(j == 0), stop=(j == CH - 1))
                            last.then_inc(window_ready, 1)
                    passes(pe, slow, body)

                windows(0)
                for layer in range(4):
                    left = layer_in[layer]
                    pe.wait_ge(tin_ready, layer + 1)
                    for g, kind, k, q in plan[layer]:
                        if k >= 0 and g - TBANKS >= plan[layer][0][0]:
                            pe.wait_ge(*evacuated(g - TBANKS))
                        bank = g % TBANKS
                        if kind == "table" and layer < 2:
                            for t in range(4 * k, min(4 * k + 4, TILES)):
                                last = nc.tensor.matmul(ps[:, bank, (t % 4) * D:(t % 4 + 1) * D], left[:, t * P:(t + 1) * P],
                                                        layer_w[layer][:, :], start=True, stop=True)
                        elif kind == "table":
                            t, h = k // 2, k % 2
                            last = nc.tensor.matmul(ps[:, bank, :], left[:, t * P:(t + 1) * P],
                                                    layer_w[layer][:, 4 * h:4 * h + 4, :].rearrange("p r f -> p (r f)"),
                                                    start=True, stop=True)
                        else:
                            n = min(BANK, NP - k * BANK)
                            last = nc.tensor.matmul(ps[:, bank, 0:n], layer_self[layer][:, :], left[:, k * BANK:k * BANK + n],
                                                    start=True, stop=True)
                        last.then_inc(product_done, 1)
                    windows(layer + 1)
                    if layer % 2:
                        ln = layer // 2
                        pe.wait_ge(y_ready, ln + 1)
                        for t in range(TILES):
                            last = nc.tensor.transpose(ps[:, t // 4, (t % 4) * P:(t % 4 + 1) * P],
                                                       acc[:, t * P:(t + 1) * P], ident[:, :])
                            if t % 4 == 3 or t == TILES - 1:
                                last.then_inc(y_turned, 1)
                        if ln == 0:
                            for g in range(XG):
                                last_t = min(4 * g + 4, TILES)
                                pe.wait_ge(normed, last_t)
                                for t in range(4 * g, last_t):
                                    last = nc.tensor.transpose(ps[:, g, (t % 4) * P:(t % 4 + 1) * P], xn[:, t, :], ident[:, :])
                                last.then_inc(xn_turned, 1)

            fast = pe.value_load(flag_i[0:1, 0:1], min_val=0, max_val=1)
            with pe.If(fast):
                rest(False)
            with pe.Else():
                rest(True)

        @block.vector
        def _(dve):
            steps = [0]

            def then(ins):
                steps[0] += 1
                ins.then_inc(dve_step, 1)
                dve.wait_ge(dve_step, steps[0])

            nc.vector.memset(xn[:, TILES - 1, :], 0.0).then_inc(x_cleared, 1)
            nc.vector.memset(ones[:, :], 1.0)
            nc.vector.memset(eps[:, :], LN_EPS)
            dve.wait_ge(edges_loaded, 9 * 16)
            nc.vector.tensor_copy(dst_f[:, :], dst_i[:, :]).then_inc(edges_float, 1)
            nc.vector.tensor_copy(src_f[:, :], src_i[:, :]).then_inc(edges_float, 1)
            then(nc.vector.tensor_copy(row_f[:, :], rel_i[:, :]))
            nc.vector.scalar_tensor_tensor(out=row_f[:, :], in0=src_f[:, :], scalar=float(R), in1=row_f[:, :],
                                           op0=ALU.mult, op1=ALU.add).then_inc(edges_float, 1)
            then(nc.vector.tensor_scalar(dst_i.bitcast(f32)[:, :] if False else inside[:, :], dst_f[:, :], dst_f[:, 0:1], None, ALU.subtract))
            then(nc.vector.tensor_scalar(src_i[:, :], inside[:, :], 0.0, None, ALU.is_ge))
            then(nc.vector.scalar_tensor_tensor(out=inside[:, :], in0=inside[:, :], scalar=float(W), in1=src_i[:, :],
                                                op0=ALU.is_lt, op1=ALU.mult))
            nc.vector.reduce_sum(inside_n[:, :], inside[:, :], AX.X).then_inc(edges_float, 1)
            for a, tile in enumerate((dst_t, src_t, row_t)):
                for h in range(2):
                    dve.wait_ge(edges_turned, 2 * a + h + 1)
                    nc.vector.tensor_copy(tile[:, 4 * h:4 * h + 4, :].rearrange("p c b -> p (c b)"), ps[:, 2 * a + h, 0:4 * NB])
            dve.wait_ge(counted, 2)
            nc.vector.tensor_copy(base_i[:, :], ps[0:1, 6, 0:NB])
            nc.vector.tensor_scalar(flag_i[:, :], ps[0:1, 7, 0:1], float(E), None, ALU.is_equal).then_inc(mode_ready, 1)
            dve.wait_ge(gate_ready, 1)
            then(nc.vector.scalar_tensor_tensor(out=shift[:, :], in0=cols[:, 1:2], scalar=gate[:, 0:1], in1=ps[:, 7, 1:2],
                                                op0=ALU.mult, op1=ALU.add))
            nc.vector.memset(dinv[:, :], 1.0).then_inc(window_free, 2)
            nc.vector.tensor_copy(eps[:, :], eps[:, :]).then_inc(gate_ready, 1)
            dve.wait_ge(node_id_ready, 1)
            dve.wait_ge(mode_ready, 1)
            steps_before = steps[0]

            def rest(slow):
                steps[0] = steps_before
                n_loop = per_loop(slow)

                def windows(loop, total):
                    def body(k, before, base):
                        bases = [base if slow else dve.value_load(base_i[0:1, bass.ds(2 * k + u, 1)], min_val=0, max_val=N_NODES - 1)
                                 for u in range(2)]
                        for u in range(2):
                            nc.vector.tensor_tensor(
                                onehot[:, u, :, :], dst_t[:, :, bass.ds(2 * k + u, 1)].to_broadcast([P, CH, W]),
                                node_id[:, bass.ds(bases[u], W)].unsqueeze(1).to_broadcast([P, CH, W]), ALU.is_equal).then_inc(onehot_ready, 1)
                        for u in range(2):
                            n = before + 2 * k + u + loop * n_loop
                            dve.wait_ge(window_ready, n + 1)
                            dve.wait_ge(window_free, n + 2)
                            part = total[:, bass.ds(bases[u], W)]
                            nc.vector.tensor_tensor(part, part, ps[:, WIN_BANK + u, 0:W], ALU.add).then_inc(window_free, 1)
                    passes(dve, slow, body)
                    dve.wait_ge(window_free, (loop + 1) * n_loop + 2)

                windows(0, dinv)
                nc.vector.tensor_scalar(dinv[:, :], dinv[:, :], 1.0, None, ALU.max).then_inc(deg_ready, 1)
                dve.wait_ge(deg_sqrt, 1)
                then(nc.vector.reciprocal(dinv[:, :], dinv[:, :]))
                dve.wait_ge(x_copied, XG)
                nc.vector.tensor_tensor(tin[:, :], xT[:, :], dinv[:, :], ALU.mult).then_inc(tin_ready, 1)
                for layer in range(4):
                    for g, kind, k, q in plan[layer]:
                        if g % 2:
                            continue
                        dve.wait_ge(product_done, g + 1)
                        if kind == "table":
                            n = table_view(layer, k)[1]
                            if q >= STAGES:
                                dve.wait_ge(stored[q % STAGES], 16 * (q // STAGES))
                            nc.vector.tensor_copy(stage[:, q % STAGES, 0:n], ps[:, g % TBANKS, 0:n]).then_inc(dve_evac, 1)
                        else:
                            n = min(BANK, NP - k * BANK)
                            dstp = acc[:, k * BANK:k * BANK + n]
                            if layer < 2:
                                nc.vector.tensor_copy(dstp, ps[:, g % TBANKS, 0:n]).then_inc(dve_evac, 1)
                            else:
                                nc.vector.tensor_scalar(dstp, ps[:, g % TBANKS, 0:n], cols[:, 1 + layer:2 + layer], None,
                                                        ALU.add).then_inc(dve_evac, 1)
                    g_end = plan[layer][-1][0]
                    for g in (g_end - 1, g_end):
                        dve.wait_ge(*evacuated(g))
                    windows(layer + 1, acc)
                    if layer == 0:
                        then(nc.vector.tensor_tensor(acc[:, :], acc[:, :], dinv[:, :], ALU.mult))
                        then(nc.vector.tensor_scalar(acc[:, :], acc[:, :], cols[:, 0:1], None, ALU.add))
                        then(nc.vector.scalar_tensor_tensor(out=acc[:, :], in0=acc[:, :], scalar=SLOPE, in1=acc[:, :],
                                                            op0=ALU.mult, op1=ALU.max))
                        nc.vector.tensor_tensor(tin[:, :], acc[:, :], dinv[:, :], ALU.mult).then_inc(tin_ready, 1)
                        continue
                    if layer == 2:
                        nc.vector.tensor_scalar(tin[:, :], acc[:, :], 0.0, None, ALU.max).then_inc(tin_ready, 1)
                        continue
                    ln = layer // 2
                    if ln == 0:
                        then(nc.vector.tensor_tensor(acc[:, :], acc[:, :], dinv[:, :], ALU.mult))
                        then(nc.vector.tensor_scalar(acc[:, :], acc[:, :], gate[:, 0:1], shift[:, 0:1], ALU.mult, ALU.add))
                        nc.vector.tensor_tensor(acc[:, :], acc[:, :], xT[:, :], ALU.add).then_inc(y_ready, 1)
                    else:
                        nc.vector.scalar_tensor_tensor(out=acc[:, :], in0=acc[:, :], scalar=0.0, in1=xT[:, :],
                                                       op0=ALU.max, op1=ALU.add).then_inc(y_ready, 1)
                    for t in range(TILES):
                        dve.wait_ge(y_turned, ln * XG + t // 4 + 1)
                        last = nc.vector.bn_stats(stats[:, t, :], ps[:, t // 4, (t % 4) * P:(t % 4 + 1) * P])
                    then(last)
                    for t in range(TILES):
                        last = nc.vector.bn_aggr(mv[:, t, :], stats[:, t, :])
                    then(last)
                    dve.sem_inc(var_ready, 1)
                    dve.wait_ge(std_ready, ln + 1)
                    then(nc.vector.reciprocal(rstd[:, :], std[:, :]))
                    for t in range(TILES):
                        nc.vector.tensor_scalar(xn[:, t, :], ps[:, t // 4, (t % 4) * P:(t % 4 + 1) * P], mv[:, t, 0:1],
                                                rstd[:, t:t + 1], ALU.subtract, ALU.mult).then_inc(normed, 1)
                    if ln == 0:
                        for g in range(XG):
                            n = min(4, TILES - 4 * g) * P
                            dve.wait_ge(xn_turned, g + 1)
                            last = nc.vector.tensor_copy(xT[:, g * BANK:g * BANK + n], ps[:, g, 0:n])
                        last.then_inc(tin_ready, 1)

            fast = dve.value_load(flag_i[0:1, 0:1], min_val=0, max_val=1)
            with dve.If(fast):
                rest(False)
            with dve.Else():
                rest(True)


_INS = ['x', 'src', 'dst', 'edge_type_8', 'L0_gnn_ctx', 'L0_gnn_W1', 'L0_gnn_b1', 'L0_gnn_W2', 'L0_gnn_b2', 'L0_gnn_Wg',
        'L0_gnn_bg', 'L0_gnn_Wb', 'L1_gnn_w1', 'L1_gnn_sl1', 'L1_gnn_b1', 'L1_gnn_w2', 'L1_gnn_sl2', 'L1_gnn_b2']


def kernel(**inputs):
    import numpy as _np
    import concourse.bacc as _bacc
    from concourse import mybir as _mybir
    from concourse.bass_utils import run_bass_kernel_spmd as _run

    nc = _bacc.Bacc("TRN2", target_bir_lowering=False, num_devices=1)
    arrays, args = {}, {}
    for name in _INS:
        a = _np.ascontiguousarray(inputs[name])
        arrays[f"in_{name}"] = a
        args[name] = nc.dram_tensor(f"in_{name}", a.shape, _mybir.dt.from_np(a.dtype), kind="ExternalInput").ap()
    out = nc.dram_tensor("out_0", (N_NODES, D), _mybir.dt.float32, kind="ExternalOutput").ap()
    gnn_kernel(nc, *[args[n] for n in _INS], out)
    r = _run(nc, [arrays], core_ids=[0])
    return r.results[0]["out_0"]
```

```python
import concourse.bass as bass
from concourse import mybir
from contextlib import ExitStack

N_NODES, D, R, CTX = 3125, 128, 8, 64
E = 100000
P = 128
TILES = -(-N_NODES // P)
NP = TILES * P
LAST = N_NODES - (TILES - 1) * P
BATCH = 1024
CH = BATCH // P
NB = -(-E // BATCH)
TAIL = E - (NB - 1) * BATCH
W = 64
PASSES = NP // W
NO_NODE = 8191
LN_EPS = 1e-5
SLOPE = 0.2
BANK = 512
STAGES = 8
TBANKS = 6
WIN_BANK = 6
STRIP = 16
STRIPS = NP // STRIP
STRIP_CH = 6
DVE_LOWS = 3
CELLS = STRIP * TILES
NBLK = -(-NP // BANK)
FULL = 96
PARTS = 3
DST, SRC, ROW, KEY, LOW, EDGE_ARRAYS = range(6)
assert NB % 2 == 0 and NP % W == 0 and CELLS <= BANK and NB * EDGE_ARRAYS <= BANK and STRIP_CH * P < 2048


def block_width(b):
    return min(BANK, NP - b * BANK)


def products(slow):
    plan, g, q = [], 0, 0
    for layer in range(4):
        rows = []
        if slow or layer >= 2:
            for kind, n in (("table", -(-TILES // 4) if layer < 2 else 2 * TILES), ("self", NBLK)):
                for k in range(n):
                    rows.append((g, kind, k, q))
                    g += 1
                    q += kind == "table"
        plan.append(rows)
    return plan


def gnn_kernel(nc, x, src, dst, rel, ctx_in, W1, b1, W2, b2, Wg, bg, Wb, w1, sl1, rb1, w2, sl2, rb2, out):
    f32, i32, f16, bf16 = mybir.dt.float32, mybir.dt.int32, mybir.dt.float16, mybir.dt.bfloat16
    ALU, ACT, AX = mybir.AluOpType, mybir.ActivationFunctionType, mybir.AxisListType

    table_gcn = nc.dram_tensor("table_gcn", (NP, D), f32).ap()
    table_rel = nc.dram_tensor("table_rel", (NP * R, D), f32).ap()
    counts_dram = [nc.dram_tensor(f"counts{b}", (P, TILES, block_width(b)), f16).ap() for b in range(NBLK)]

    with ExitStack() as stack:
        def sb(name, shape, dt=f32):
            return stack.enter_context(nc.sbuf_tensor(name, shape, dt))

        def sem(name):
            return stack.enter_context(nc.semaphore(name))

        raw = sb("raw", [P, 8, BATCH])
        dst_i, src_i, rel_i = (raw[0:NB, a, :].bitcast(i32) for a in range(3))
        edge_f = raw[0:NB, 3:8, :]
        inside = raw[0:NB, 2, :]
        nonneg = raw[0:NB, 1, :]
        parts = raw[:, 0:5, :].rearrange("p a e -> p (a e)")[:, 0:PARTS * NP // 2].bitcast(bf16)\
            .rearrange("p (c t f) -> p c t f", c=PARTS, t=TILES)
        rest = raw[:, 5:7, :].rearrange("p a (h e) -> p (a h) e", h=2)
        inside_n = sb("inside_n", [NB, 1])
        edges = sb("edges", [P, EDGE_ARRAYS, NB, CH])
        base_i = sb("base_i", [1, NB], i32)
        start_f = sb("start_f", [1, STRIPS])
        start_i = sb("start_i", [1, STRIPS], i32)
        flag_i = sb("flag_i", [1, 1], i32)
        sums = sb("sums", [1, 2])
        ident = sb("ident", [P, P])
        ones = sb("ones", [P, P])
        ones_h = sb("ones_h", [P, P], f16)
        node_id = sb("node_id", [P, NP])
        strip_node = sb("strip_node", [P, STRIPS])
        strip_key = sb("strip_key", [P, STRIPS])
        cell_h = sb("cell_h", [P, CELLS], f16)
        xn = sb("xn", [P, TILES, D])
        xT = sb("xT", [P, NP])
        tin = sb("tin", [P, NP])
        acc = sb("acc", [P, NP])
        started = acc[0:NB, 0:CH * STRIPS].rearrange("b (c s) -> b c s", c=CH)
        dinv = sb("dinv", [P, NP])
        blocks = sb("blocks", [P, 2, TILES * BANK], f16)
        loop_mem = blocks[:, :, :].rearrange("p a b -> p (a b)").bitcast(f32)

        def carve(at, n):
            return loop_mem[:, at:at + n]

        stage = carve(0, STAGES * BANK).rearrange("p (s n) -> p s n", s=STAGES)
        onehot = carve(4096, 2 * CH * W).rearrange("p (u c w) -> p u c w", u=2, c=CH)
        msgs = carve(5120, 2 * CH * D).rearrange("p (u c f) -> p u c f", u=2, c=CH)
        idx = sb("idx", [P, 2, CH], i32)
        strip_keys = sb("strip_keys", [P, 2, STRIP_CH])
        low_gap = sb("low_gap", [P, 2, STRIP_CH - DVE_LOWS, P], f16)
        low_hot = sb("low_hot", [P, 2, STRIP_CH, P], f16)
        cell_hot = sb("cell_hot", [P, 2, STRIP_CH, CELLS], f16)
        wg1, wg2, ws1, ws2 = (sb(n, [P, D]) for n in ("wg1", "wg2", "ws1", "ws2"))
        wr1, wr2 = (sb(n, [P, R, D]) for n in ("wr1", "wr2"))
        wgate, wbias = (sb(n, [CTX, D]) for n in ("wgate", "wbias"))
        cols = sb("cols", [P, 5])
        ctx_c = sb("ctx_c", [CTX, 1])
        gate = sb("gate", [P, 1])
        shift = sb("shift", [P, 1])
        eps = sb("eps", [P, 1])
        stats = sb("stats", [P, TILES, 6])
        mv = sb("mv", [P, TILES, 2])
        std = sb("std", [P, TILES])
        rstd = sb("rstd", [P, TILES])
        ps = stack.enter_context(nc.psum_tensor("ps", [P, 8, BANK], f32))

        edges_cleared, x_cleared = sem("edges_cleared"), sem("x_cleared")
        edges_loaded, x_loaded, weights_loaded = sem("edges_loaded"), sem("x_loaded"), sem("weights_loaded")
        pool_step, ident_ready, patterns_ready = sem("pool_step"), sem("ident_ready"), sem("patterns_ready")
        dve_step = sem("dve_step")
        edges_ready, edges_turned, edges_copied = sem("edges_ready"), sem("edges_turned"), sem("edges_copied")
        inside_ready, started_ready, sums_ready = sem("inside_ready"), sem("started_ready"), sem("sums_ready")
        sums_read, starts_ready, keys_ready = sem("sums_read"), sem("starts_ready"), sem("keys_ready")
        x_turned, x_copied = sem("x_turned"), sem("x_copied")
        gate_product, gate_ready, shift_ready = sem("gate_product"), sem("gate_ready"), sem("shift_ready")
        gaps_ready, lows_ready = sem("gaps_ready"), sem("lows_ready")
        hots_ready, strip_counted, strip_copied = sem("hots_ready"), sem("strip_counted"), sem("strip_copied")
        degrees_ready, degrees_read = sem("degrees_ready"), sem("degrees_read")
        counts_stored = [sem(f"counts_stored{u}") for u in range(2)]
        counts_loaded = [sem(f"counts_loaded{u}") for u in range(2)]
        mode_ready = sem("mode_ready")
        deg_ready, deg_sqrt, tin_ready = sem("deg_ready"), sem("deg_sqrt"), sem("tin_ready")
        feat_done, high_ready, rest_ready, mid_ready, low_ready = (
            sem(n) for n in ("feat_done", "high_ready", "rest_ready", "mid_ready", "low_ready"))
        block_summed, block_read = sem("block_summed"), sem("block_read")
        onehot_ready, window_ready, window_free = sem("onehot_ready"), sem("window_ready"), sem("window_free")
        idx_ready = sem("idx_ready")
        gathered = [sem(f"gathered{u}") for u in range(2)]
        product_done, dve_evac, act_evac = sem("product_done"), sem("dve_evac"), sem("act_evac")
        stored = [sem(f"stored{u}") for u in range(STAGES)]
        y_ready, y_turned, var_ready, std_ready = sem("y_ready"), sem("y_turned"), sem("var_ready"), sem("std_ready")
        normed, xn_turned = sem("normed"), sem("xn_turned")
        out_stored = sem("out_stored")

        XG = -(-TILES // 4)
        EDGE_LOADS = 9
        W_LOADS = 14
        STARTS_BANK, SUMS_BANK = 6, 7
        DEG_BANK = 4
        layer_in = [tin, tin, xT, tin]
        layer_w = [wg1, wg2, wr1, wr2]
        layer_self = [wg1, wg2, ws1, ws2]

        def evacuated(g):
            return (act_evac if g % 2 else dve_evac), g // 2 + 1

        def table_view(layer, k):
            if layer < 2:
                n = min(4, TILES - 4 * k)
                return table_gcn.rearrange("(t p) f -> p t f", p=P)[:, 4 * k:4 * k + n, :], n * D
            t, h = k // 2, k % 2
            return table_rel.rearrange("(t p r) f -> p t (r f)", p=P, r=R)[:, t, h * BANK:(h + 1) * BANK], BANK

        def block_of(b):
            return blocks[:, b % 2, 0:TILES * block_width(b)].rearrange("p (t n) -> p t n", t=TILES)

        def node_tiles(b):
            return range(4 * b, min(4 * b + 4, TILES))

        def for_batches(eng, slow, body):
            if slow:
                with eng.Fori(0, PASSES) as p:
                    with eng.Fori(0, NB // 2) as k:
                        body(k, p * NB, p * W)
            else:
                with eng.Fori(0, NB // 2) as k:
                    body(k, 0, None)

        def loop_batches(slow):
            return NB * (PASSES if slow else 1)

        def gather_layers(slow):
            return range(0 if slow else 2, 4)

        chunk_of = [edges[:, a, :, :].rearrange("p b c -> p (b c)") for a in range(EDGE_ARRAYS)]

        def load_row(eng, row, first, n, last):
            return nc.values_load_multi_w_load_instructions(
                row[0:1, bass.ds(first, n)], engines=[eng.engine], min_val=0, max_val=last,
                skip_runtime_bounds_check_because="they are node numbers of the input, or clamped by VectorE")[1]

        def branch(eng, rest_of):
            fast = eng.value_load(flag_i[0:1, 0:1], min_val=0, max_val=1)
            with eng.If(fast):
                rest_of(False)
            with eng.Else():
                rest_of(True)

        block = stack.enter_context(nc.Block())

        @block.sync
        def _(sp):
            sp.wait_ge(edges_cleared, 3)
            for dram, tile in ((dst, dst_i), (src, src_i), (rel, rel_i)):
                sp.dma_start(tile[0:FULL, :], dram[0:FULL * BATCH].rearrange("(b e) -> b e", e=BATCH)).then_inc(edges_loaded, 16)
                sp.dma_start(tile[FULL:NB - 1, :], dram[FULL * BATCH:(NB - 1) * BATCH].rearrange("(b e) -> b e", e=BATCH)).then_inc(edges_loaded, 16)
                sp.dma_start(tile[NB - 1:NB, 0:TAIL], dram[(NB - 1) * BATCH:E].rearrange("(b e) -> b e", b=1)).then_inc(edges_loaded, 16)
            for tile, dram in ((wg1, W1), (wg2, W2), (ws1, sl1), (ws2, sl2), (wgate, Wg), (wbias, Wb)):
                sp.dma_start(tile[:, :], dram).then_inc(weights_loaded, 16)
            for tile, dram in ((wr1, w1), (wr2, w2)):
                sp.dma_start(tile[:, :, :], dram.rearrange("r d e -> d r e")).then_inc(weights_loaded, 16)
            for c, dram in enumerate((b1, b2, bg, rb1, rb2)):
                sp.dma_start(cols[:, c:c + 1], dram.rearrange("(p a) -> p a", a=1)).then_inc(weights_loaded, 16)
            sp.dma_start(ctx_c[:, :], ctx_in.rearrange("a c -> c a")).then_inc(weights_loaded, 16)
            for b in range(NBLK):
                sp.wait_ge(strip_copied, 2 + min(STRIPS, (b + 1) * BANK // STRIP))
                sp.dma_start(counts_dram[b][:, :, :].rearrange("p t n -> p (t n)"),
                             blocks[:, b % 2, 0:TILES * block_width(b)]).then_inc(counts_stored[b % 2], 16)

            def rest_of(slow):
                if not slow:
                    for u in range(2):
                        sp.wait_ge(counts_stored[u], 16 * len(range(u, NBLK, 2)))
                    for layer in range(2):
                        for b in range(NBLK):
                            i = layer * NBLK + b
                            if i >= 2:
                                sp.wait_ge(block_summed, i - 1)
                            else:
                                sp.wait_ge(degrees_ready, NBLK)
                            sp.dma_start(blocks[:, i % 2, 0:TILES * block_width(b)],
                                         counts_dram[b][:, :, :].rearrange("p t n -> p (t n)")).then_inc(counts_loaded[i % 2], 16)
                for layer in gather_layers(slow):
                    for g, kind, k, q in products(slow)[layer]:
                        if kind == "table":
                            view, n = table_view(layer, k)
                            sp.wait_ge(*evacuated(g))
                            rows = stage[:, q % STAGES, 0:n]
                            if layer < 2:
                                rows = rows.rearrange("p (t f) -> p t f", f=D)
                            sp.dma_start(view, rows).then_inc(stored[q % STAGES], 16)
                sp.wait_ge(normed, 2 * TILES)
                sp.dma_start(out[0:(TILES - 1) * P, :].rearrange("(t p) f -> p t f", p=P), xn[:, 0:TILES - 1, :]).then_inc(out_stored, 16)
                sp.dma_start(out[(TILES - 1) * P:N_NODES, :], xn[0:LAST, TILES - 1, :]).then_inc(out_stored, 16)
                sp.wait_ge(out_stored, 32)

            sp.wait_ge(mode_ready, 1)
            branch(sp, rest_of)

        @block.gpsimd
        def _(pool):
            for tile, pad in ((dst_i, NO_NODE), (src_i, 0), (rel_i, 0)):
                nc.gpsimd.memset(tile, pad).then_inc(edges_cleared, 1)
            nc.gpsimd.memset(ident[:, :], 0.0).then_inc(pool_step, 1)
            pool.wait_ge(pool_step, 1)
            nc.gpsimd.affine_select(out=ident[:, :], in_=ident[:, :], compare_op=ALU.not_equal, fill=1.0, base=0,
                                    pattern=[[-1, P]], channel_multiplier=1).then_inc(ident_ready, 1)
            for tile, step, n in ((strip_node, STRIP, STRIPS), (strip_key, CELLS, STRIPS), (cell_h, 1, CELLS), (node_id, 1, NP)):
                nc.gpsimd.iota(tile[:, :], pattern=[[step, n]], base=0, channel_multiplier=0,
                               allow_small_or_imprecise_dtypes=True).then_inc(patterns_ready, 1)

            def rest_of(slow):
                plan = products(slow)
                for loop, layer in enumerate(gather_layers(slow)):
                    table = table_gcn if layer < 2 else table_rel
                    stores = 1 + max(q for _, kind, _, q in plan[layer] if kind == "table")
                    for s in range(STAGES):
                        pool.wait_ge(stored[s], 16 * len(range(s, stores, STAGES)))

                    def body(k, before, base):
                        for u in range(2):
                            n = before + 2 * k + u + loop * loop_batches(slow)
                            pool.wait_ge(idx_ready, n + 1)
                            pool.nop(nofuse=True)
                            for j in range(CH):
                                nc.gpsimd.indirect_dma_start(
                                    msgs[:, u, j, :], None, table,
                                    bass.IndirectOffsetOnAxis(ap=idx[:, u, j:j + 1], axis=0)).then_inc(gathered[u], 16)
                    for_batches(pool, slow, body)

            pool.wait_ge(mode_ready, 1)
            branch(pool, rest_of)

        @block.scalar
        def _(act):
            act.wait_ge(x_cleared, 1)
            act.dma_start(xn[:, 0:TILES - 1, :], x[0:(TILES - 1) * P, :].rearrange("(t p) f -> p t f", p=P)).then_inc(x_loaded, 16)
            act.dma_start(xn[0:LAST, TILES - 1, :], x[(TILES - 1) * P:N_NODES, :]).then_inc(x_loaded, 16)
            act.wait_ge(starts_ready, 1)
            act.wait_ge(patterns_ready, 4)
            for b in range(NBLK):
                if b >= 2:
                    act.wait_ge(degrees_ready, b - 1)
                    act.wait_ge(counts_stored[b % 2], 16 * (b // 2))
                view = block_of(b)

                def evacuate(k, u):
                    act.wait_ge(strip_counted, b * (BANK // STRIP) + 2 * k + u + 3)
                    nc.scalar.activation(view[:, :, bass.ds(32 * k + STRIP * u, STRIP)],
                                         ps[:, u, 0:CELLS].rearrange("p (n t) -> p t n", t=TILES), ACT.Copy).then_inc(strip_copied, 1)

                def lows(k, u, start):
                    strip = b * (BANK // STRIP) + 2 * k + u
                    act.wait_ge(lows_ready, strip + 1)
                    for c in range(DVE_LOWS, STRIP_CH):
                        last = nc.scalar.activation(low_gap[:, u, c - DVE_LOWS, :], cell_h[:, 0:P], ACT.Abs,
                                                    bias=chunk_of[LOW][:, bass.ds(start + c, 1)])
                    last.then_inc(gaps_ready, 1)
                    act.wait_ge(gaps_ready, strip + 1)
                    act.wait_ge(strip_counted, strip + 1)
                    nc.scalar.activation(low_hot[:, u, DVE_LOWS:STRIP_CH, :], low_gap[:, u, :, :], ACT.Relu, scale=-1.0, bias=1.0)\
                        .then_inc(lows_ready, 1)

                pairs = block_width(b) // STRIP // 2
                starts = load_row(act, start_i, b * (BANK // STRIP), 2, NB * CH - STRIP_CH)
                lows(0, 0, starts[0])
                lows(0, 1, starts[1])
                with act.Fori(1, pairs) as k:
                    starts = load_row(act, start_i, b * (BANK // STRIP) + 2 * k, 2, NB * CH - STRIP_CH)
                    for u in range(2):
                        evacuate(k - 1, u)
                        lows(k, u, starts[u])
                for u in range(2):
                    evacuate(pairs - 1, u)
            for g in range(XG):
                n = block_width(g)
                act.wait_ge(x_turned, g + 1)
                nc.scalar.activation(xT[:, g * BANK:g * BANK + n], ps[:, g, 0:n], ACT.Copy).then_inc(x_copied, 1)
            act.wait_ge(gate_product, 1)
            nc.scalar.activation(gate[:, :], ps[:, 7, 0:1], ACT.Sigmoid, bias=cols[:, 2:3]).then_inc(gate_ready, 1)

            def rest_of(slow):
                plan = products(slow)
                act.wait_ge(deg_ready, 1)
                nc.scalar.activation(dinv[:, :], dinv[:, :], ACT.Sqrt).then_inc(deg_sqrt, 1)
                if not slow:
                    for layer in range(2):
                        for g in range(XG):
                            i, tiles = layer * XG + g, node_tiles(g)
                            feats = ps[:, g % 4, 0:len(tiles) * D]
                            part = [parts[:, c, tiles[0]:tiles[-1] + 1, :].rearrange("p t f -> p (t f)") for c in range(PARTS)]
                            act.wait_ge(feat_done, i + 1)
                            if i >= XG:
                                act.wait_ge(block_summed, NBLK)
                            nc.scalar.activation(part[0], feats, ACT.Copy).then_inc(high_ready, 1)
                            act.wait_ge(rest_ready, i + 1)
                            nc.scalar.activation(part[1], rest[:, g % 4, 0:len(tiles) * D], ACT.Copy).then_inc(mid_ready, 1)
                        if layer:
                            act.wait_ge(var_ready, 1)
                            nc.scalar.activation(std[:, :], mv[:, :, 1], ACT.Sqrt, bias=eps[:, 0:1]).then_inc(std_ready, 1)
                for loop, layer in enumerate(gather_layers(slow)):
                    for g, kind, k, q in plan[layer]:
                        if g % 2 == 0:
                            continue
                        act.wait_ge(product_done, g + 1)
                        if kind == "table":
                            n = table_view(layer, k)[1]
                            if q >= STAGES:
                                act.wait_ge(stored[q % STAGES], 16 * (q // STAGES))
                            nc.scalar.activation(stage[:, q % STAGES, 0:n], ps[:, g % TBANKS, 0:n], ACT.Copy).then_inc(act_evac, 1)
                        else:
                            n = block_width(k)
                            own = acc[:, k * BANK:k * BANK + n]
                            if layer < 2:
                                nc.scalar.activation(own, ps[:, g % TBANKS, 0:n], ACT.Copy).then_inc(act_evac, 1)
                            else:
                                nc.scalar.activation(own, ps[:, g % TBANKS, 0:n], ACT.Identity,
                                                     bias=cols[:, 1 + layer:2 + layer]).then_inc(act_evac, 1)

                    def body(k, before, base):
                        for u in range(2):
                            n = before + 2 * k + u + (loop + slow) * loop_batches(slow)
                            act.wait_ge(window_free, n + 1)
                            nc.scalar.activation(idx[:, u, :], edges[:, SRC if layer < 2 else ROW, bass.ds(2 * k + u, 1), :]
                                                 .rearrange("p a c -> p (a c)"), ACT.Copy).then_inc(idx_ready, 1)
                    for_batches(act, slow, body)
                    if layer % 2:
                        norm = layer // 2
                        act.wait_ge(var_ready, norm + 1)
                        nc.scalar.activation(std[:, :], mv[:, :, 1], ACT.Sqrt, bias=eps[:, 0:1]).then_inc(std_ready, 1)

            act.wait_ge(mode_ready, 1)
            branch(act, rest_of)

        @block.tensor
        def _(pe):
            pe.wait_ge(ident_ready, 1)
            pe.wait_ge(edges_ready, 1)
            for c in range(CH):
                for a in range(EDGE_ARRAYS):
                    last = nc.tensor.transpose(ps[:, c, a * NB:(a + 1) * NB], edge_f[:, a, c * P:(c + 1) * P], ident[0:NB, 0:NB])
                last.then_inc(edges_turned, 1)
            pe.wait_ge(edges_copied, CH)
            pe.wait_ge(started_ready, 1)
            for c in range(CH):
                last = nc.tensor.matmul(ps[0:1, STARTS_BANK, 0:STRIPS], ones[0:NB, 0:1], started[:, c, :], start=(c == 0), stop=(c == CH - 1))
            last.then_inc(sums_ready, 1)
            nc.tensor.matmul(ps[0:1, SUMS_BANK, 0:NB], edge_f[:, DST, 0:1], ident[0:NB, 0:NB], start=True, stop=True)
            pe.wait_ge(inside_ready, 1)
            nc.tensor.matmul(ps[0:1, SUMS_BANK, NB:NB + 1], inside_n[:, 0:1], ones[0:NB, 0:1], start=True, stop=True).then_inc(sums_ready, 1)
            for b in range(NBLK):
                with pe.Fori(0, block_width(b) // STRIP // 2) as k:
                    for u in range(2):
                        strip = b * (BANK // STRIP) + 2 * k + u
                        pe.wait_ge(strip_copied, strip + 1)
                        pe.wait_ge(hots_ready, strip + 3)
                        pe.wait_ge(lows_ready, strip + 3)
                        for c in range(STRIP_CH):
                            last = nc.tensor.matmul(ps[:, u, 0:CELLS], low_hot[:, u, c, :], cell_hot[:, u, c, :],
                                                    start=(c == 0), stop=(c == STRIP_CH - 1))
                        last.then_inc(strip_counted, 1)
                pe.wait_ge(strip_copied, 2 + min(STRIPS, (b + 1) * BANK // STRIP))
                if b >= 2:
                    pe.wait_ge(degrees_read, b - 1)
                for t in range(TILES):
                    last = nc.tensor.matmul(ps[:, DEG_BANK + b % 2, 0:block_width(b)], ones_h[:, :], block_of(b)[:, t, :],
                                            start=(t == 0), stop=(t == TILES - 1))
                last.then_inc(degrees_ready, 1)
            pe.wait_ge(degrees_read, NBLK)
            pe.wait_ge(sums_read, 1)
            pe.wait_ge(x_loaded, 32)
            for t in range(TILES):
                last = nc.tensor.transpose(ps[:, t // 4, (t % 4) * P:(t % 4 + 1) * P], xn[:, t, :], ident[:, :])
                if t % 4 == 3 or t == TILES - 1:
                    last.then_inc(x_turned, 1)
            pe.wait_ge(weights_loaded, 16 * W_LOADS)
            nc.tensor.matmul(ps[:, 7, 0:1], wgate[:, :], ctx_c[:, :], start=True, stop=True)
            nc.tensor.matmul(ps[:, 7, 1:2], wbias[:, :], ctx_c[:, :], start=True, stop=True).then_inc(gate_product, 1)
            pe.wait_ge(shift_ready, 1)

            def rest_of(slow):
                plan = products(slow)

                def windows(loop, gathers):
                    def body(k, before, base):
                        for u in range(2):
                            n = before + 2 * k + u + loop * loop_batches(slow)
                            pe.wait_ge(window_free, n + 1)
                            pe.wait_ge(onehot_ready, n + 1)
                            if gathers is not None:
                                pairs = (base * (NB // 2 // 2) // (W // 2) if slow else 0) + k
                                pe.wait_ge(gathered[u], pairs * (16 * CH) + (gathers * loop_batches(slow) // 2 + 1) * 16 * CH)
                            for j in range(CH):
                                left = ones[:, :] if gathers is None else msgs[:, u, j, :]
                                last = nc.tensor.matmul(ps[:, WIN_BANK + u, 0:W], left, onehot[:, u, j, :],
                                                        start=(j == 0), stop=(j == CH - 1))
                            last.then_inc(window_ready, 1)
                    for_batches(pe, slow, body)

                def turn_y():
                    for t in range(TILES):
                        last = nc.tensor.transpose(ps[:, t // 4, (t % 4) * P:(t % 4 + 1) * P],
                                                   acc[:, t * P:(t + 1) * P], ident[:, :])
                        if t % 4 == 3 or t == TILES - 1:
                            last.then_inc(y_turned, 1)

                def turn_back():
                    for g in range(XG):
                        pe.wait_ge(normed, node_tiles(g)[-1] + 1)
                        for t in node_tiles(g):
                            last = nc.tensor.transpose(ps[:, g, (t % 4) * P:(t % 4 + 1) * P], xn[:, t, :], ident[:, :])
                        last.then_inc(xn_turned, 1)

                if slow:
                    windows(0, None)
                else:
                    for layer in range(2):
                        pe.wait_ge(tin_ready, layer + 1)
                        for g in range(XG):
                            i = layer * XG + g
                            if i >= 4:
                                pe.wait_ge(rest_ready, i - 3 if g >= 4 else layer * XG)
                            for t in node_tiles(g):
                                last = nc.tensor.matmul(ps[:, g % 4, (t % 4) * D:(t % 4 + 1) * D], tin[:, t * P:(t + 1) * P],
                                                        layer_w[layer][:, :], start=True, stop=True)
                            last.then_inc(feat_done, 1)
                        pe.wait_ge(low_ready, (layer + 1) * XG)
                        pe.wait_ge(mid_ready, (layer + 1) * XG)
                        for b in range(NBLK):
                            i, n = layer * NBLK + b, block_width(b)
                            total = ps[:, DEG_BANK + i % 2, 0:n]
                            if i >= 2:
                                pe.wait_ge(block_read, i - 1)
                            nc.tensor.matmul(total, layer_self[layer][:, :], tin[:, b * BANK:b * BANK + n], start=True, stop=False)
                            pe.wait_ge(counts_loaded[i % 2], 16 * (i // 2 + 1))
                            for t in range(TILES):
                                for c in range(PARTS):
                                    last = nc.tensor.matmul(total, parts[:, c, t, :],
                                                            blocks[:, i % 2, t * n:(t + 1) * n],
                                                            start=False, stop=(t == TILES - 1 and c == PARTS - 1))
                            last.then_inc(block_summed, 1)
                    pe.wait_ge(y_ready, 1)
                    turn_y()
                    turn_back()
                for loop, layer in enumerate(gather_layers(slow)):
                    left = layer_in[layer]
                    pe.wait_ge(tin_ready, layer + 1)
                    for g, kind, k, q in plan[layer]:
                        if g - TBANKS >= plan[layer][0][0]:
                            pe.wait_ge(*evacuated(g - TBANKS))
                        bank = g % TBANKS
                        if kind == "self":
                            n = block_width(k)
                            last = nc.tensor.matmul(ps[:, bank, 0:n], layer_self[layer][:, :], left[:, k * BANK:k * BANK + n],
                                                    start=True, stop=True)
                        elif layer < 2:
                            for t in node_tiles(k):
                                last = nc.tensor.matmul(ps[:, bank, (t % 4) * D:(t % 4 + 1) * D], left[:, t * P:(t + 1) * P],
                                                        layer_w[layer][:, :], start=True, stop=True)
                        else:
                            t, h = k // 2, k % 2
                            last = nc.tensor.matmul(ps[:, bank, :], left[:, t * P:(t + 1) * P],
                                                    layer_w[layer][:, 4 * h:4 * h + 4, :].rearrange("p r f -> p (r f)"),
                                                    start=True, stop=True)
                        last.then_inc(product_done, 1)
                    windows(loop + slow, loop)
                    if layer % 2:
                        pe.wait_ge(y_ready, layer // 2 + 1)
                        turn_y()
                        if layer == 1:
                            turn_back()

            pe.wait_ge(mode_ready, 1)
            branch(pe, rest_of)

        @block.vector
        def _(dve):
            steps = [0]

            def then(ins):
                steps[0] += 1
                ins.then_inc(dve_step, 1)
                dve.wait_ge(dve_step, steps[0])

            nc.vector.memset(xn[:, TILES - 1, :], 0.0).then_inc(x_cleared, 1)
            nc.vector.memset(ones[:, :], 1.0)
            nc.vector.memset(ones_h[:, :], 1.0)
            nc.vector.memset(eps[:, :], LN_EPS)
            dve.sem_inc(window_free, 2)
            dve.sem_inc(lows_ready, 2)
            dve.sem_inc(hots_ready, 2)
            dve.sem_inc(strip_counted, 2)
            dve.sem_inc(strip_copied, 2)
            dve.wait_ge(edges_loaded, EDGE_LOADS * 16)
            f = [edge_f[:, a, :] for a in range(EDGE_ARRAYS)]
            then(nc.vector.tensor_scalar(f[KEY].bitcast(i32), src_i, 7, None, ALU.logical_shift_right))
            then(nc.vector.tensor_copy(f[LOW], f[KEY].bitcast(i32)))
            nc.vector.tensor_copy(f[DST], dst_i)
            nc.vector.tensor_copy(f[SRC], src_i)
            then(nc.vector.tensor_copy(f[ROW], rel_i))
            then(nc.vector.scalar_tensor_tensor(out=f[KEY], in0=f[DST], scalar=float(-TILES), in1=f[LOW], op0=ALU.mult, op1=ALU.subtract))
            nc.vector.scalar_tensor_tensor(out=f[ROW], in0=f[SRC], scalar=float(R), in1=f[ROW], op0=ALU.mult, op1=ALU.add)
            then(nc.vector.scalar_tensor_tensor(out=f[LOW], in0=f[LOW], scalar=float(P), in1=f[SRC], op0=ALU.mult, op1=ALU.subtract))
            dve.sem_inc(edges_ready, 1)
            for c in range(CH):
                dve.wait_ge(edges_turned, c + 1)
                nc.vector.tensor_copy(edges[:, :, :, c], ps[:, c, 0:EDGE_ARRAYS * NB].rearrange("p (a b) -> p a b", a=EDGE_ARRAYS))\
                    .then_inc(edges_copied, 1)
            dve.wait_ge(patterns_ready, 4)
            for c in range(CH):
                last = nc.vector.tensor_scalar(started[:, c, :], strip_node[0:NB, :], f[DST][:, c * P:c * P + 1], None, ALU.is_gt)
            last.then_inc(started_ready, 1)
            then(nc.vector.tensor_scalar(inside, f[DST], f[DST][:, 0:1], None, ALU.subtract))
            then(nc.vector.tensor_scalar(nonneg, inside, 0.0, None, ALU.is_ge))
            then(nc.vector.scalar_tensor_tensor(out=inside, in0=inside, scalar=float(W), in1=nonneg, op0=ALU.is_lt, op1=ALU.mult))
            nc.vector.reduce_sum(inside_n[:, :], inside, AX.X).then_inc(inside_ready, 1)
            dve.wait_ge(sums_ready, 1)
            then(nc.vector.tensor_scalar(start_f[:, :], ps[0:1, STARTS_BANK, 0:STRIPS], -1.0, 0.0, ALU.add, ALU.max))
            nc.vector.tensor_scalar(start_i[:, :], start_f[:, :], float(NB * CH - STRIP_CH), None, ALU.min).then_inc(starts_ready, 1)
            dve.wait_ge(sums_ready, 2)
            nc.vector.tensor_copy(base_i[:, :], ps[0:1, SUMS_BANK, 0:NB])
            then(nc.vector.tensor_copy(sums[:, 0:1], ps[0:1, SUMS_BANK, NB:NB + 1]))
            dve.sem_inc(sums_read, 1)
            dve.wait_ge(edges_copied, CH)
            dve.wait_ge(starts_ready, 1)
            for b in range(NBLK):
                with dve.Fori(0, block_width(b) // STRIP // 2) as k:
                    first = b * (BANK // STRIP) + 2 * k
                    starts = load_row(dve, start_i, first, 2, NB * CH - STRIP_CH)
                    dve.wait_ge(hots_ready, first + 2)
                    for u in range(2):
                        nc.vector.tensor_scalar(strip_keys[:, u, :], chunk_of[KEY][:, bass.ds(starts[u], STRIP_CH)],
                                                strip_key[:, bass.ds(first + u, 1)], None, ALU.add).then_inc(keys_ready, 1)
                    for u in range(2):
                        dve.wait_ge(keys_ready, first + u + 1)
                        dve.wait_ge(strip_counted, first + u + 1)
                        for c in range(DVE_LOWS):
                            nc.vector.tensor_scalar(low_hot[:, u, c, :], cell_h[:, 0:P], chunk_of[LOW][:, bass.ds(starts[u] + c, 1)],
                                                    0.0, ALU.add, ALU.is_equal)
                        for c in range(STRIP_CH):
                            last = nc.vector.tensor_scalar(cell_hot[:, u, c, :], cell_h[:, :], strip_keys[:, u, c:c + 1],
                                                           0.0, ALU.add, ALU.is_equal)
                        last.then_inc(hots_ready, 1)
                dve.wait_ge(degrees_ready, b + 1)
                nc.vector.tensor_scalar(dinv[:, b * BANK:b * BANK + block_width(b)], ps[:, DEG_BANK + b % 2, 0:block_width(b)],
                                        1.0, None, ALU.add).then_inc(degrees_read, 1)
            dve.wait_ge(degrees_read, NBLK)
            then(nc.vector.reduce_sum(sums[:, 1:2], dinv[0:1, :], AX.X))
            then(nc.vector.tensor_scalar(sums[:, 1:2], sums[:, 1:2], float(-NP), None, ALU.add))
            then(nc.vector.tensor_tensor(sums[:, 0:1], sums[:, 0:1], sums[:, 1:2], ALU.min))
            nc.vector.tensor_scalar(flag_i[:, :], sums[:, 0:1], float(E), None, ALU.is_equal).then_inc(mode_ready, 1)
            dve.wait_ge(gate_ready, 1)
            nc.vector.scalar_tensor_tensor(out=shift[:, :], in0=cols[:, 1:2], scalar=gate[:, 0:1], in1=ps[:, 7, 1:2],
                                           op0=ALU.mult, op1=ALU.add).then_inc(shift_ready, 1)
            dve.wait_ge(x_copied, XG)
            dve.wait_ge(mode_ready, 1)
            steps_before = steps[0]

            def rest_of(slow):
                steps[0] = steps_before
                plan = products(slow)

                def windows(loop, total):
                    def body(k, before, base):
                        bases = [base, base] if slow else load_row(dve, base_i, 2 * k, 2, N_NODES - 1)
                        for u in range(2):
                            nc.vector.tensor_tensor(
                                onehot[:, u, :, :],
                                edges[:, DST, bass.ds(2 * k + u, 1), :].rearrange("p a c -> p (a c)").unsqueeze(2).to_broadcast([P, CH, W]),
                                node_id[:, bass.ds(bases[u], W)].unsqueeze(1).to_broadcast([P, CH, W]),
                                ALU.is_equal).then_inc(onehot_ready, 1)
                        for u in range(2):
                            n = before + 2 * k + u + loop * loop_batches(slow)
                            dve.wait_ge(window_ready, n + 1)
                            dve.wait_ge(window_free, n + 2)
                            part = total[:, bass.ds(bases[u], W)]
                            nc.vector.tensor_tensor(part, part, ps[:, WIN_BANK + u, 0:W], ALU.add).then_inc(window_free, 1)
                    for_batches(dve, slow, body)
                    dve.wait_ge(window_free, (loop + 1) * loop_batches(slow) + 2)

                def layer_norm(norm):
                    for t in range(TILES):
                        dve.wait_ge(y_turned, norm * XG + t // 4 + 1)
                        last = nc.vector.bn_stats(stats[:, t, :], ps[:, t // 4, (t % 4) * P:(t % 4 + 1) * P])
                    then(last)
                    for t in range(TILES):
                        last = nc.vector.bn_aggr(mv[:, t, :], stats[:, t, :])
                    last.then_inc(var_ready, 1)
                    dve.wait_ge(std_ready, norm + 1)
                    then(nc.vector.reciprocal(rstd[:, :], std[:, :]))
                    for t in range(TILES):
                        nc.vector.tensor_scalar(xn[:, t, :], ps[:, t // 4, (t % 4) * P:(t % 4 + 1) * P], mv[:, t, 0:1],
                                                rstd[:, t:t + 1], ALU.subtract, ALU.mult).then_inc(normed, 1)

                def copy_back():
                    for g in range(XG):
                        n = block_width(g)
                        dve.wait_ge(xn_turned, g + 1)
                        last = nc.vector.tensor_copy(xT[:, g * BANK:g * BANK + n], ps[:, g, 0:n])
                    last.then_inc(tin_ready, 1)

                def first_layer_end(sums_, cut):
                    then(nc.vector.tensor_tensor(acc[:, cut], sums_, dinv[:, cut], ALU.mult))
                    then(nc.vector.tensor_scalar(acc[:, cut], acc[:, cut], cols[:, 0:1], None, ALU.add))
                    then(nc.vector.scalar_tensor_tensor(out=acc[:, cut], in0=acc[:, cut], scalar=SLOPE, in1=acc[:, cut],
                                                        op0=ALU.mult, op1=ALU.max))
                    return nc.vector.tensor_tensor(tin[:, cut], acc[:, cut], dinv[:, cut], ALU.mult)

                def second_layer_end(sums_, cut):
                    then(nc.vector.tensor_tensor(acc[:, cut], sums_, dinv[:, cut], ALU.mult))
                    then(nc.vector.tensor_scalar(acc[:, cut], acc[:, cut], gate[:, 0:1], shift[:, 0:1], ALU.mult, ALU.add))
                    return nc.vector.tensor_tensor(acc[:, cut], acc[:, cut], xT[:, cut], ALU.add)

                everything = slice(0, NP)
                if slow:
                    then(nc.vector.memset(dinv[:, :], 1.0))
                    windows(0, dinv)
                nc.vector.tensor_scalar(dinv[:, :], dinv[:, :], 1.0, None, ALU.max).then_inc(deg_ready, 1)
                dve.wait_ge(deg_sqrt, 1)
                then(nc.vector.reciprocal(dinv[:, :], dinv[:, :]))
                nc.vector.tensor_tensor(tin[:, :], xT[:, :], dinv[:, :], ALU.mult).then_inc(tin_ready, 1)
                if not slow:
                    for layer in range(2):
                        for g in range(XG):
                            i, tiles = layer * XG + g, node_tiles(g)
                            n = len(tiles) * D
                            part = [parts[:, c, tiles[0]:tiles[-1] + 1, :].rearrange("p t f -> p (t f)") for c in range(PARTS)]
                            dve.wait_ge(high_ready, i + 1)
                            nc.vector.tensor_tensor(rest[:, g % 4, 0:n], ps[:, g % 4, 0:n], part[0], ALU.subtract).then_inc(rest_ready, 1)
                            dve.wait_ge(mid_ready, i + 1)
                            nc.vector.tensor_tensor(part[2], rest[:, g % 4, 0:n], part[1], ALU.subtract).then_inc(low_ready, 1)
                        for b in range(NBLK):
                            i, n = layer * NBLK + b, block_width(b)
                            cut = slice(b * BANK, b * BANK + n)
                            dve.wait_ge(block_summed, i + 1)
                            end = (second_layer_end if layer else first_layer_end)(ps[:, DEG_BANK + i % 2, 0:n], cut)
                            end.then_inc(block_read, 1)
                        dve.wait_ge(block_read, (layer + 1) * NBLK)
                        dve.sem_inc(y_ready if layer else tin_ready, 1)
                    layer_norm(0)
                    copy_back()
                for loop, layer in enumerate(gather_layers(slow)):
                    for g, kind, k, q in plan[layer]:
                        if g % 2:
                            continue
                        dve.wait_ge(product_done, g + 1)
                        if kind == "table":
                            n = table_view(layer, k)[1]
                            if q >= STAGES:
                                dve.wait_ge(stored[q % STAGES], 16 * (q // STAGES))
                            nc.vector.tensor_copy(stage[:, q % STAGES, 0:n], ps[:, g % TBANKS, 0:n]).then_inc(dve_evac, 1)
                        else:
                            n = block_width(k)
                            own = acc[:, k * BANK:k * BANK + n]
                            if layer < 2:
                                nc.vector.tensor_copy(own, ps[:, g % TBANKS, 0:n]).then_inc(dve_evac, 1)
                            else:
                                nc.vector.tensor_scalar(own, ps[:, g % TBANKS, 0:n], cols[:, 1 + layer:2 + layer], None,
                                                        ALU.add).then_inc(dve_evac, 1)
                    for g in (plan[layer][-2][0], plan[layer][-1][0]):
                        dve.wait_ge(*evacuated(g))
                    windows(loop + slow, acc)
                    if layer == 0:
                        first_layer_end(acc[:, :], everything).then_inc(tin_ready, 1)
                    elif layer == 1:
                        second_layer_end(acc[:, :], everything).then_inc(y_ready, 1)
                        layer_norm(0)
                        copy_back()
                    elif layer == 2:
                        nc.vector.tensor_scalar(tin[:, :], acc[:, :], 0.0, None, ALU.max).then_inc(tin_ready, 1)
                    else:
                        nc.vector.scalar_tensor_tensor(out=acc[:, :], in0=acc[:, :], scalar=0.0, in1=xT[:, :],
                                                       op0=ALU.max, op1=ALU.add).then_inc(y_ready, 1)
                        layer_norm(1)

            branch(dve, rest_of)


_INS = ['x', 'src', 'dst', 'edge_type_8', 'L0_gnn_ctx', 'L0_gnn_W1', 'L0_gnn_b1', 'L0_gnn_W2', 'L0_gnn_b2', 'L0_gnn_Wg',
        'L0_gnn_bg', 'L0_gnn_Wb', 'L1_gnn_w1', 'L1_gnn_sl1', 'L1_gnn_b1', 'L1_gnn_w2', 'L1_gnn_sl2', 'L1_gnn_b2']


def kernel(**inputs):
    import numpy as _np
    import concourse.bacc as _bacc
    from concourse import mybir as _mybir
    from concourse.bass_utils import run_bass_kernel_spmd as _run

    nc = _bacc.Bacc("TRN2", target_bir_lowering=False, num_devices=1)
    arrays, args = {}, {}
    for name in _INS:
        a = _np.ascontiguousarray(inputs[name])
        arrays[f"in_{name}"] = a
        args[name] = nc.dram_tensor(f"in_{name}", a.shape, _mybir.dt.from_np(a.dtype), kind="ExternalInput").ap()
    out = nc.dram_tensor("out_0", (N_NODES, D), _mybir.dt.float32, kind="ExternalOutput").ap()
    gnn_kernel(nc, *[args[n] for n in _INS], out)
    r = _run(nc, [arrays], core_ids=[0])
    return r.results[0]["out_0"]
```

```python
import concourse.bass as bass
from concourse import mybir
from contextlib import ExitStack

N_NODES, D, R, CTX = 3125, 128, 8, 64
E = 100000
P = 128
TILES = -(-N_NODES // P)
NP = TILES * P
LAST = N_NODES - (TILES - 1) * P
BATCH = 1024
CH = BATCH // P
NB = -(-E // BATCH)
TAIL = E - (NB - 1) * BATCH
W = 64
PASSES = NP // W
NO_NODE = 8191
LN_EPS = 1e-5
SLOPE = 0.2
BANK = 512
STAGES = 8
TBANKS = 6
WIN_BANK = 6
STRIP = 16
STRIPS = NP // STRIP
STRIP_CH = 6
DVE_LOWS = 3
CELLS = STRIP * TILES
NBLK = -(-NP // BANK)
FULL = 96
PARTS = 3
HALF = 32
HCOLS = HALF * R
RSTRIP = 4
RSTRIP_CH = 3
RCELLS = RSTRIP * R * TILES
HSTRIPS = HALF // RSTRIP
TURNS = 10
SLOTS2, SLOTS3 = 8, 6
MADE2, USED2, USED3 = 4, 2, 4
HALVES = TURNS * MADE2
SPLIT3 = -(-N_NODES // HALF) * HALF - HALVES * HALF
SPLIT2 = SPLIT3 + TURNS * (MADE2 - USED2) * HALF
BATCHES2, BATCHES3 = TURNS * SLOTS2, TURNS * SLOTS3
RSTRIPS = HALVES * HSTRIPS
RKEYS = R * TILES
DST, ROW, KEY, LOW, RKEY, EDGE_ARRAYS = range(6)
assert USED2 == 2 and USED3 == 4
assert NB % 2 == 0 and NP % W == 0 and CELLS <= BANK and NB * EDGE_ARRAYS <= BANK and STRIP_CH * P < 2048


def block_width(b):
    return min(BANK, NP - b * BANK)


def products(slow):
    plan, g, q = [], 0, 0
    for layer in range(4):
        rows = []
        if slow or layer >= 2:
            for kind, n in (("table", -(-TILES // 4) if layer < 2 else 2 * TILES), ("self", NBLK)):
                for k in range(n):
                    rows.append((g, kind, k, q))
                    g += 1
                    q += kind == "table"
        plan.append(rows)
    return plan


def gnn_kernel(nc, x, src, dst, rel, ctx_in, W1, b1, W2, b2, Wg, bg, Wb, w1, sl1, rb1, w2, sl2, rb2, out):
    f32, i32, f16, bf16 = mybir.dt.float32, mybir.dt.int32, mybir.dt.float16, mybir.dt.bfloat16
    ALU, ACT, AX = mybir.AluOpType, mybir.ActivationFunctionType, mybir.AxisListType

    table_gcn = nc.dram_tensor("table_gcn", (NP, D), f32).ap()
    table_rel = nc.dram_tensor("table_rel", (NP * R, D), f32).ap()
    rcounts_dram = nc.dram_tensor("rcounts", (HALVES, P, TILES * HCOLS), f16).ap()
    counts_dram = [nc.dram_tensor(f"counts{b}", (P, TILES, block_width(b)), f16).ap() for b in range(NBLK)]

    with ExitStack() as stack:
        def sb(name, shape, dt=f32):
            return stack.enter_context(nc.sbuf_tensor(name, shape, dt))

        def sem(name):
            return stack.enter_context(nc.semaphore(name))

        raw = sb("raw", [P, 8, BATCH])
        dst_i, src_i, rel_i = (raw[0:NB, a, :].bitcast(i32) for a in range(3))
        edge_f = raw[0:NB, 3:8, :]
        inside = raw[0:NB, 2, :]
        nonneg = raw[0:NB, 1, :]
        parts = raw[:, 0:5, :].rearrange("p a e -> p (a e)")[:, 0:PARTS * NP // 2].bitcast(bf16)\
            .rearrange("p (c t f) -> p c t f", c=PARTS, t=TILES)
        rest = raw[:, 5:7, :].rearrange("p a (h e) -> p (a h) e", h=2)
        row_sums = sb("row_sums", [NB, 2])
        edges = sb("edges", [P, EDGE_ARRAYS, NB, CH])
        base_i = sb("base_i", [1, 1 + NB], i32)
        rstart_i = sb("rstart_i", [1, RSTRIPS], i32)
        start_i = sb("start_i", [1, STRIPS + 2], i32)
        flag_i = sb("flag_i", [1, 1], i32)
        sums = sb("sums", [1, 4])
        ident = sb("ident", [P, P])
        ones = sb("ones", [P, P])
        ones_h = sb("ones_h", [P, P], f16)
        node_id = sb("node_id", [P, NP + W])
        strip_key = sb("strip_key", [P, STRIPS + 2])
        rstrip_key = sb("rstrip_key", [P, RSTRIPS])
        cell_h = sb("cell_h", [P, RCELLS], f16)
        xn = sb("xn", [P, TILES, D])
        xT = sb("xT", [P, NP])
        strip_node = xT[:, 0:STRIPS]
        rstrip_node = xT[:, BANK:BANK + RSTRIPS + 1]
        start_f = xT[0:1, 2 * BANK:2 * BANK + STRIPS]
        rstart_f = xT[0:1, 3 * BANK:3 * BANK + RSTRIPS]
        faults = xT[0:1, 4 * BANK:4 * BANK + RSTRIPS + NB - 1 + 2]
        firsts = xT[0:1, 5 * BANK:5 * BANK + NB]
        tin = sb("tin", [P, NP])
        acc = sb("acc", [P, NP + W])
        started = acc[0:NB, 0:CH * STRIPS].rearrange("b (c s) -> b c s", c=CH)
        rstarted = tin[0:NB, 0:CH * (RSTRIPS + 1)].rearrange("b (c s) -> b c s", c=CH)
        dinv = sb("dinv", [P, NP])
        blocks = sb("blocks", [P, 2, TILES * BANK], f16)
        loop_mem = blocks[:, :, :].rearrange("p a b -> p (a b)").bitcast(f32)

        def carve(at, n):
            return loop_mem[:, at:at + n]

        stage = carve(0, STAGES * BANK).rearrange("p (s n) -> p s n", s=STAGES)
        halves = blocks[:, :, :].rearrange("p a b -> p (a b)").rearrange("p (j n) -> p j n", j=MADE2)
        relsum = raw[:, 7, 0:2 * HCOLS].rearrange("p (u n) -> p u n", u=2)

        def onehot_of(slow):
            at = carve(4096, 2 * CH * W) if slow else raw[:, 6, :]
            return at.rearrange("p (u c w) -> p u c w", u=2, c=CH)

        def msgs_of(slow):
            if slow:
                flat = [carve(5120 + u * CH * D, CH * D) for u in range(2)]
            else:
                flat = [dinv[:, u * CH * D:(u + 1) * CH * D] for u in range(3)] + [raw[:, 5, :]]
            return [m.rearrange("p (c f) -> p c f", c=CH) for m in flat]

        idx = sb("idx", [P, 4, CH], i32)
        strip_keys = sb("strip_keys", [P, 4, STRIP_CH])
        low_gap = sb("low_gap", [P, 2, STRIP_CH - DVE_LOWS, P], f16)
        low_hot = sb("low_hot", [P, 2, STRIP_CH, P], f16)
        cell_hot = sb("cell_hot", [P, 2, STRIP_CH, CELLS], f16)
        rcell_hot = cell_hot[:, :, :, :].rearrange("p u c n -> p u (c n)").rearrange("p u (c n) -> p u c n", c=RSTRIP_CH)
        wg1, wg2, ws1, ws2 = (sb(n, [P, D]) for n in ("wg1", "wg2", "ws1", "ws2"))
        wr1, wr2 = (sb(n, [P, R, D]) for n in ("wr1", "wr2"))
        wgate, wbias = (sb(n, [CTX, D]) for n in ("wgate", "wbias"))
        cols = sb("cols", [P, 5])
        ctx_c = sb("ctx_c", [CTX, 1])
        gate = sb("gate", [P, 1])
        shift = sb("shift", [P, 1])
        eps = sb("eps", [P, 1])
        dinv_col = sb("dinv_col", [P, TILES])
        stats = sb("stats", [P, TILES, 6])
        mv = sb("mv", [P, TILES, 2])
        std = sb("std", [P, TILES])
        rstd = sb("rstd", [P, TILES])
        ps = stack.enter_context(nc.psum_tensor("ps", [P, 8, BANK], f32))

        edges_cleared, x_cleared = sem("edges_cleared"), sem("x_cleared")
        edges_loaded, x_loaded, weights_loaded = sem("edges_loaded"), sem("x_loaded"), sem("weights_loaded")
        pool_step, ident_ready, patterns_ready = sem("pool_step"), sem("ident_ready"), sem("patterns_ready")
        dve_step = sem("dve_step")
        edges_ready, edges_turned, edges_copied = sem("edges_ready"), sem("edges_turned"), sem("edges_copied")
        inside_ready, started_ready, sums_ready = sem("inside_ready"), sem("started_ready"), sem("sums_ready")
        sums_read, starts_ready, keys_ready = sem("sums_read"), sem("starts_ready"), sem("keys_ready")
        x_turned, x_copied = sem("x_turned"), sem("x_copied")
        gate_product, gate_ready, shift_ready = sem("gate_product"), sem("gate_ready"), sem("shift_ready")
        gaps_ready, lows_ready = sem("gaps_ready"), sem("lows_ready")
        hots_ready, strip_counted, strip_copied = sem("hots_ready"), sem("strip_counted"), sem("strip_copied")
        degrees_ready, degrees_read, degrees_sqrt = sem("degrees_ready"), sem("degrees_read"), sem("degrees_sqrt")
        counts_stored = [sem(f"counts_stored{u}") for u in range(2)]
        counts_loaded = [sem(f"counts_loaded{u}") for u in range(2)]
        mode_ready = sem("mode_ready")
        deg_ready, deg_sqrt, tin_ready = sem("deg_ready"), sem("deg_sqrt"), sem("tin_ready")
        diag_ready, dinv_spread, dinv_copied, scaled = (sem(n) for n in ("diag_ready", "dinv_spread", "dinv_copied", "scaled"))
        feat_done, high_ready, rest_ready, mid_ready, low_ready = (
            sem(n) for n in ("feat_done", "high_ready", "rest_ready", "mid_ready", "low_ready"))
        block_summed, block_read = sem("block_summed"), sem("block_read")
        onehot_ready, window_ready, window_free = sem("onehot_ready"), sem("window_ready"), sem("window_free")
        idx_ready = sem("idx_ready")
        passes_done = sem("passes_done")
        gathered = [sem(f"gathered{u}") for u in range(4)]
        halves_stored = [sem(f"halves_stored{j}") for j in range(MADE2)]
        halves_loaded = [sem(f"halves_loaded{j}") for j in range(MADE2)]
        rel_summed, rel_copied, rel_out, rel_added = (sem(n) for n in ("rel_summed", "rel_copied", "rel_out", "rel_added"))
        product_done, dve_evac, act_evac = sem("product_done"), sem("dve_evac"), sem("act_evac")
        stored = [sem(f"stored{u}") for u in range(STAGES)]
        y_ready, y_turned, var_ready, std_ready = sem("y_ready"), sem("y_turned"), sem("var_ready"), sem("std_ready")
        normed, xn_turned, xT_copied = sem("normed"), sem("xn_turned"), sem("xT_copied")
        out_stored = sem("out_stored")

        XG = -(-TILES // 4)
        OUT_TILES = ((0, 12), (12, 20), (20, TILES - 1))
        EDGE_LOADS = 9
        W_LOADS = 14
        RSTARTS_BANK, STARTS_BANK, SUMS_BANK = 3, 6, 7
        SHARES = 5
        CTX_BANK = 7
        DEG_BANK = 4
        layer_in = [tin, tin, xT, tin]
        layer_w = [wg1, wg2, wr1, wr2]
        layer_self = [wg1, wg2, ws1, ws2]

        def evacuated(g):
            return (act_evac if g % 2 else dve_evac), g // 2 + 1

        def table_view(layer, k):
            if layer < 2:
                n = min(4, TILES - 4 * k)
                return table_gcn.rearrange("(t p) f -> p t f", p=P)[:, 4 * k:4 * k + n, :], n * D
            t, h = k // 2, k % 2
            return table_rel.rearrange("(t p r) f -> p t (r f)", p=P, r=R)[:, t, h * BANK:(h + 1) * BANK], BANK

        def block_of(b):
            return blocks[:, b % 2, 0:TILES * block_width(b)].rearrange("p (t n) -> p t n", t=TILES)

        def node_tiles(b):
            return range(4 * b, min(4 * b + 4, TILES))

        def for_batches(eng, body):
            with eng.Fori(0, PASSES) as p:
                with eng.Fori(0, NB // 2) as k:
                    body(k, p)

        def gather_layers(slow):
            return range(0 if slow else 2, 4)

        chunk_of = [edges[:, a, :, :].rearrange("p b c -> p (b c)") for a in range(EDGE_ARRAYS)]

        def load_row(eng, row, first, n, last):
            return nc.values_load_multi_w_load_instructions(
                row[0:1, bass.ds(first, n)], engines=[eng.engine], min_val=0, max_val=last,
                skip_runtime_bounds_check_because="they are node numbers of the input, or clamped by VectorE")[1]

        def blocks_stored(eng):
            for u in range(2):
                eng.wait_ge(counts_stored[u], 16 * len(range(u, NBLK, 2)))

        def tables_stored(eng, slow, layer):
            stores = 1 + max(q for _, kind, _, q in products(slow)[layer] if kind == "table")
            for s in range(STAGES):
                eng.wait_ge(stored[s], 16 * len(range(s, stores, STAGES)))

        LOOP_BATCHES = NB * PASSES

        SUMMED, WINDOWS = 4, 4

        def half_number(i, j):
            return TURNS * (MADE2 - USED2) + USED2 * i + j if j < USED2 else (MADE2 - USED2) * i + j - USED2

        def parts_of(tiles):
            return [parts[:, c, tiles[0]:tiles[-1] + 1, :].rearrange("p t f -> p (t f)") for c in range(PARTS)]

        def features(layer, g):
            if layer == 2:
                return xn[:, node_tiles(g)[0]:node_tiles(g)[-1] + 1, :].rearrange("p t f -> p (t f)")
            return ps[:, WIN_BANK + g % 2 if layer == 3 else g % 4, 0:block_width(g)]

        NORM_AT = (4, 8, 12)

        def norms_before(slow, norm):
            return norm * (1 if slow else XG)

        def split_steps_at(g):
            return [step for step in range(XG + 1) if 3 * step + 4 + (g + step) % 2 == g]

        def use_of(layer, s):
            n = TILES * PARTS
            if layer == 2:
                a, b = ([0, 0, 0, n // 3, 2 * n // 3, n, n * 3 // 2, 2 * n, 2 * n][t] for t in (s, s + 1))
            else:
                a, b = s * n * USED3 // SLOTS3, (s + 1) * n * USED3 // SLOTS3
            return [(j, max(a - j * n, 0), min(b - j * n, n)) for j in range(MADE2) if a < (j + 1) * n and b > j * n]

        def pairs_of(layer, s):
            return [j for j, _, end in use_of(layer, s) if end == TILES * PARTS and j % 2]

        def quarter(layer, s, q):
            ks = [(j, k) for j, a, b in use_of(layer, s) for k in range(a, b)]
            return ks[len(ks) * q // 4:len(ks) * (q + 1) // 4]

        def branch(eng, rest_of):
            fast = eng.value_load(flag_i[0:1, 0:1], min_val=0, max_val=1)
            with eng.If(fast):
                rest_of(False)
            with eng.Else():
                rest_of(True)

        block = stack.enter_context(nc.Block())

        @block.sync
        def _(sp):
            sp.wait_ge(edges_cleared, 3)
            for dram, tile in ((dst, dst_i), (src, src_i), (rel, rel_i)):
                sp.dma_start(tile[0:FULL, :], dram[0:FULL * BATCH].rearrange("(b e) -> b e", e=BATCH)).then_inc(edges_loaded, 16)
                sp.dma_start(tile[FULL:NB - 1, :], dram[FULL * BATCH:(NB - 1) * BATCH].rearrange("(b e) -> b e", e=BATCH)).then_inc(edges_loaded, 16)
                sp.dma_start(tile[NB - 1:NB, 0:TAIL], dram[(NB - 1) * BATCH:E].rearrange("(b e) -> b e", b=1)).then_inc(edges_loaded, 16)
            for tile, dram in ((wg1, W1), (wg2, W2), (ws1, sl1), (ws2, sl2), (wgate, Wg), (wbias, Wb)):
                sp.dma_start(tile[:, :], dram).then_inc(weights_loaded, 16)
            for tile, dram in ((wr1, w1), (wr2, w2)):
                sp.dma_start(tile[:, :, :], dram.rearrange("r d e -> d r e")).then_inc(weights_loaded, 16)
            for c, dram in enumerate((b1, b2, bg, rb1, rb2)):
                sp.dma_start(cols[:, c:c + 1], dram.rearrange("(p a) -> p a", a=1)).then_inc(weights_loaded, 16)
            sp.dma_start(ctx_c[:, :], ctx_in.rearrange("a c -> c a")).then_inc(weights_loaded, 16)
            for b in range(NBLK):
                sp.wait_ge(strip_copied, 2 + min(STRIPS, (b + 1) * BANK // STRIP))
                sp.dma_start(counts_dram[b][:, :, :].rearrange("p t n -> p (t n)"),
                             blocks[:, b % 2, 0:TILES * block_width(b)]).then_inc(counts_stored[b % 2], 16)

            def rest_of(slow):
                if not slow:
                    blocks_stored(sp)
                    for layer in range(2):
                        for b in range(NBLK):
                            i = layer * NBLK + b
                            if i >= 2:
                                sp.wait_ge(block_summed, i - 1)
                            else:
                                sp.wait_ge(degrees_ready, NBLK)
                            sp.dma_start(blocks[:, i % 2, 0:TILES * block_width(b)],
                                         counts_dram[b][:, :, :].rearrange("p t n -> p (t n)")).then_inc(counts_loaded[i % 2], 16)
                for layer in gather_layers(slow):
                    if layer == 3 and not slow:
                        with sp.Fori(0, TURNS) as i:
                            for j in range(MADE2):
                                sp.wait_ge(strip_copied, 2 + STRIPS + MADE2 * HSTRIPS * i + HSTRIPS * (j + 1))
                                sp.dma_start(rcounts_dram[bass.ds(half_number(i, j), 1), :, :].rearrange("a p n -> p (a n)"),
                                             halves[:, j, :]).then_inc(halves_stored[j], 16)
                    for g, kind, k, q in products(slow)[layer]:
                        if kind == "table":
                            view, n = table_view(layer, k)
                            sp.wait_ge(*evacuated(g))
                            rows = stage[:, q % STAGES, 0:n]
                            if layer < 2:
                                rows = rows.rearrange("p (t f) -> p t f", f=D)
                            sp.dma_start(view, rows).then_inc(stored[q % STAGES], 16)
                    if layer == 3 and not slow:
                        for j in range(MADE2):
                            sp.wait_ge(halves_stored[j], 16 * (TURNS + 1))
                        tables_stored(sp, slow, layer)
                        sp.wait_ge(rel_summed, SUMMED + TURNS * USED2)
                        with sp.Fori(0, TURNS) as i:
                            for j in range(USED3):
                                sp.wait_ge(rel_summed, SUMMED + TURNS * USED2 + USED3 * i - USED3 + j + 1)
                                sp.dma_start(halves[:, j, :], rcounts_dram[bass.ds(USED3 * i + j, 1), :, :].rearrange("a p n -> p (a n)"))\
                                    .then_inc(halves_loaded[j], 16)
                for first, end in OUT_TILES:
                    sp.wait_ge(normed, TILES + end)
                    sp.dma_start(out[first * P:end * P, :].rearrange("(t p) f -> p t f", p=P), xn[:, first:end, :]).then_inc(out_stored, 16)
                sp.wait_ge(normed, 2 * TILES)
                sp.dma_start(out[(TILES - 1) * P:N_NODES, :], xn[0:LAST, TILES - 1, :]).then_inc(out_stored, 16)
                sp.wait_ge(out_stored, 16 * (len(OUT_TILES) + 1))

            sp.wait_ge(mode_ready, 1)
            branch(sp, rest_of)

        @block.gpsimd
        def _(pool):
            for tile, pad in ((dst_i, NO_NODE), (src_i, 0), (rel_i, 0)):
                nc.gpsimd.memset(tile, pad).then_inc(edges_cleared, 1)
            nc.gpsimd.memset(ident[:, :], 0.0).then_inc(pool_step, 1)
            pool.wait_ge(pool_step, 1)
            nc.gpsimd.affine_select(out=ident[:, :], in_=ident[:, :], compare_op=ALU.not_equal, fill=1.0, base=0,
                                    pattern=[[-1, P]], channel_multiplier=1).then_inc(ident_ready, 1)
            for tile, first, step, n in ((strip_node, 0, STRIP, STRIPS), (rstrip_node, SPLIT3, RSTRIP, RSTRIPS + 1),
                                         (strip_key, 0, CELLS, STRIPS + 2), (rstrip_key, SPLIT3 * RKEYS, RSTRIP * RKEYS, RSTRIPS),
                                         (cell_h, 0, 1, RCELLS), (node_id, 1, 1, NP + W)):
                nc.gpsimd.iota(tile[:, :], pattern=[[step, n]], base=first, channel_multiplier=0,
                               allow_small_or_imprecise_dtypes=True).then_inc(patterns_ready, 1)

            def rest_of(slow):
                msgs = msgs_of(slow)
                for loop, layer in enumerate(gather_layers(slow)):
                    table = table_gcn if layer < 2 else table_rel
                    tables_stored(pool, slow, layer)

                    def gather(n, u):
                        pool.wait_ge(idx_ready, n + 1)
                        pool.nop(nofuse=True)
                        for j in range(CH):
                            nc.gpsimd.indirect_dma_start(
                                msgs[u][:, j, :], None, table,
                                bass.IndirectOffsetOnAxis(ap=idx[:, u, j:j + 1], axis=0)).then_inc(gathered[u], 16)

                    if not slow:
                        pool.wait_ge(low_ready, (layer + 1) * XG)
                        with pool.Fori(0, TURNS) as i:
                            for s in range(SLOTS2 if layer == 2 else SLOTS3):
                                if layer == 2:
                                    gather(SLOTS2 * i + s, s % 4)
                                else:
                                    gather(BATCHES2 + 3 + SLOTS3 * i + s, s % 3)
                        continue

                    with pool.Fori(0, PASSES) as p:
                        before = loop * LOOP_BATCHES + p * NB
                        with pool.Fori(0, NB // 2) as k:
                            for u in range(2):
                                gather(before + 2 * k + u, u)
                        for u in range(2):
                            pool.wait_ge(gathered[u], NB // 2 * CH * 16)
                        pool.wait_ge(window_free, LOOP_BATCHES + before + NB + 2)
                        pool.nop(nofuse=True)
                        nc.gpsimd.inc_swdge_sem(gathered[0:2], [NB // 2 * CH * 16] * 2, mode="sub")
                        pool.sem_inc(passes_done, 1)

            pool.wait_ge(mode_ready, 1)
            branch(pool, rest_of)

        @block.scalar
        def _(act):
            act.wait_ge(x_cleared, 1)
            act.dma_start(xn[:, 0:TILES - 1, :], x[0:(TILES - 1) * P, :].rearrange("(t p) f -> p t f", p=P)).then_inc(x_loaded, 16)
            act.dma_start(xn[0:LAST, TILES - 1, :], x[(TILES - 1) * P:N_NODES, :]).then_inc(x_loaded, 16)
            act.wait_ge(starts_ready, 1)
            act.wait_ge(patterns_ready, 6)
            for b in range(NBLK):
                if b >= 2:
                    act.wait_ge(degrees_ready, b - 1)
                    act.wait_ge(counts_stored[b % 2], 16 * (b // 2))
                view = block_of(b)

                def evacuate(k, u):
                    act.wait_ge(strip_counted, b * (BANK // STRIP) + 2 * k + u + 3)
                    nc.scalar.activation(view[:, :, bass.ds(32 * k + STRIP * u, STRIP)],
                                         ps[:, u, 0:CELLS].rearrange("p (n t) -> p t n", t=TILES), ACT.Copy).then_inc(strip_copied, 1)

                def lows(k, u, start):
                    strip = b * (BANK // STRIP) + 2 * k + u
                    act.wait_ge(lows_ready, strip + 1)
                    for c in range(DVE_LOWS, STRIP_CH):
                        last = nc.scalar.activation(low_gap[:, u, c - DVE_LOWS, :], cell_h[:, 0:P], ACT.Abs,
                                                    bias=chunk_of[LOW][:, bass.ds(start + c, 1)])
                    last.then_inc(gaps_ready, 1)
                    act.wait_ge(gaps_ready, strip + 1)
                    act.wait_ge(strip_counted, strip + 1)
                    nc.scalar.activation(low_hot[:, u, DVE_LOWS:STRIP_CH, :], low_gap[:, u, :, :], ACT.Relu, scale=-1.0, bias=1.0)\
                        .then_inc(lows_ready, 1)

                pairs = block_width(b) // STRIP // 2
                starts = load_row(act, start_i, b * (BANK // STRIP), 2, NB * CH - STRIP_CH)
                lows(0, 0, starts[0])
                lows(0, 1, starts[1])
                with act.Fori(1, pairs) as k:
                    starts = load_row(act, start_i, b * (BANK // STRIP) + 2 * k, 2, NB * CH - STRIP_CH)
                    for u in range(2):
                        evacuate(k - 1, u)
                        lows(k, u, starts[u])
                for u in range(2):
                    evacuate(pairs - 1, u)
            act.wait_ge(gate_product, 1)
            nc.scalar.activation(dinv_col[:, :], ps[:, CTX_BANK, 2:2 + TILES], ACT.Sqrt).then_inc(degrees_sqrt, 1)
            nc.scalar.activation(gate[:, :], ps[:, CTX_BANK, 0:1], ACT.Sigmoid, bias=cols[:, 2:3]).then_inc(gate_ready, 1)
            for g in range(XG):
                n = block_width(g)
                act.wait_ge(x_turned, g + 1)
                nc.scalar.activation(xT[:, g * BANK:g * BANK + n], ps[:, g, 0:n], ACT.Copy).then_inc(x_copied, 1)

            def rest_of(slow):
                plan = products(slow)
                if slow:
                    act.wait_ge(deg_ready, 1)
                    nc.scalar.activation(dinv[:, :], dinv[:, :], ACT.Sqrt).then_inc(deg_sqrt, 1)
                    blocks_stored(act)

                def split_step(layer, g):
                    if g < XG:
                        if layer == 2:
                            act.wait_ge(normed, node_tiles(g)[-1] + 1)
                        else:
                            act.wait_ge(feat_done, (layer - (layer == 3)) * XG + g + 1)
                        nc.scalar.activation(parts_of(node_tiles(g))[0], features(layer, g), ACT.Copy).then_inc(high_ready, 1)
                    if g:
                        act.wait_ge(rest_ready, layer * XG + g)
                        nc.scalar.activation(parts_of(node_tiles(g - 1))[1], rest[:, (g - 1) % 4, 0:block_width(g - 1)],
                                             ACT.Copy).then_inc(mid_ready, 1)

                def deviation(g):
                    tiles = slice(node_tiles(g)[0], node_tiles(g)[-1] + 1)
                    act.wait_ge(var_ready, g + 1)
                    nc.scalar.activation(std[:, tiles], mv[:, tiles, 1], ACT.Sqrt, bias=eps[:, 0:1]).then_inc(std_ready, 1)

                if not slow:
                    for g in range(XG):
                        act.wait_ge(dinv_spread, g + 1)
                        nc.scalar.activation(dinv[:, g * BANK:g * BANK + block_width(g)], ps[:, g, 0:block_width(g)], ACT.Copy)\
                            .then_inc(dinv_copied, 1)
                    for layer in range(2):
                        if layer:
                            act.wait_ge(block_summed, NBLK)
                        for g in range(XG + 1):
                            split_step(layer, g)
                        if layer:
                            for g in range(XG - 1):
                                deviation(g)
                for loop, layer in enumerate(gather_layers(slow)):
                    if layer == 3 and not slow:
                        for j in range(MADE2):
                            act.wait_ge(halves_stored[j], 16 * (TURNS + 1))
                    for g, kind, k, q in plan[layer]:
                        if g % 2 == 0:
                            continue
                        if layer == 2 and not slow and g == NORM_AT[0] + 3:
                            deviation(XG - 1)
                        if not slow:
                            for step in split_steps_at(g - plan[layer][0][0]):
                                split_step(layer, step)
                        act.wait_ge(product_done, g + 1)
                        if kind == "table":
                            n = table_view(layer, k)[1]
                            if q >= STAGES:
                                act.wait_ge(stored[q % STAGES], 16 * (q // STAGES))
                            nc.scalar.activation(stage[:, q % STAGES, 0:n], ps[:, g % TBANKS, 0:n], ACT.Copy).then_inc(act_evac, 1)
                        else:
                            n = block_width(k)
                            own = acc[:, k * BANK:k * BANK + n]
                            if layer < 2:
                                nc.scalar.activation(own, ps[:, g % TBANKS, 0:n], ACT.Copy).then_inc(act_evac, 1)
                            else:
                                nc.scalar.activation(own, ps[:, g % TBANKS, 0:n], ACT.Identity,
                                                     bias=cols[:, 1 + layer:2 + layer]).then_inc(act_evac, 1)

                    def number_rows(batch, u):
                        rows = KEY if layer < 2 else ROW
                        nc.scalar.activation(idx[:, u, :], edges[:, rows, bass.ds(batch, 1), :].rearrange("p a c -> p (a c)"),
                                             ACT.Copy).then_inc(idx_ready, 1)

                    def copy_sums(m, pair, j, bank):
                        act.wait_ge(rel_summed, SUMMED + m + 1)
                        act.wait_ge(rel_out, pair + 1)
                        nc.scalar.activation(relsum[:, j % 2, :], ps[:, bank, 0:HCOLS], ACT.Copy).then_inc(rel_copied, 1)

                    if not slow:
                        if layer == 3:
                            act.wait_ge(idx_ready, BATCHES2 + 3)
                        for n in range(3):
                            number_rows(n, n)
                        if layer == 2:
                            tables_stored(act, slow, layer)
                    if not slow and layer == 2:
                        with act.Fori(0, TURNS) as i:
                            for s in range(SLOTS2):
                                n = SLOTS2 * i + s
                                j, local = s // 2, MADE2 * HSTRIPS * i + 4 * s
                                where = half_number(i, j) * HSTRIPS + 4 * (s % 2)
                                starts = load_row(act, rstart_i, where, 4, NB * CH - RSTRIP_CH)
                                if s % 2 == 0:
                                    act.wait_ge(halves_stored[j], 16 * i + 16)
                                    if j < USED2:
                                        act.wait_ge(rel_summed, SUMMED + USED2 * i + j - USED2 + 1)

                                def rlows(q):
                                    strip, u = STRIPS + local + q, q % 2
                                    act.wait_ge(lows_ready, strip + 1)
                                    nc.scalar.activation(low_gap[:, u, 0, :], cell_h[:, 0:P], ACT.Abs,
                                                         bias=chunk_of[LOW][:, bass.ds(starts[q] + RSTRIP_CH - 1, 1)]).then_inc(gaps_ready, 1)
                                    act.wait_ge(gaps_ready, strip + 1)
                                    act.wait_ge(strip_counted, strip + 1)
                                    nc.scalar.activation(low_hot[:, u, RSTRIP_CH - 1, :], low_gap[:, u, 0, :], ACT.Relu,
                                                         scale=-1.0, bias=1.0).then_inc(lows_ready, 1)

                                def revacuate(q):
                                    u = q % 2
                                    act.wait_ge(strip_counted, STRIPS + local + q + 3)
                                    to = halves[:, j, :].rearrange("p (t r d) -> p t r d", t=TILES, r=R)
                                    for h in range(2):
                                        d = RSTRIP * (4 * (s % 2) + q) + 2 * h
                                        last = nc.scalar.activation(to[:, :, :, d:d + 2], ps[:, 2 * u + h, 0:CELLS]
                                                                    .rearrange("p (d r t) -> p t r d", d=2, r=R), ACT.Copy)
                                    last.then_inc(strip_copied, 1)

                                rlows(0)
                                rlows(1)
                                act.wait_ge(window_ready, WINDOWS + n)
                                number_rows(n + 3, (s + 3) % 4)
                                revacuate(0)
                                rlows(2)
                                revacuate(1)
                                rlows(3)
                                revacuate(2)
                                revacuate(3)
                                for jj, _, end in use_of(2, s):
                                    if end == TILES * PARTS:
                                        copy_sums(USED2 * i + jj, i + jj // 2, jj, 4)
                        continue
                    if not slow:
                        with act.Fori(0, TURNS) as i:
                            for s in range(SLOTS3):
                                for jj, _, end in use_of(3, s):
                                    if end == TILES * PARTS:
                                        copy_sums(TURNS * USED2 + USED3 * i + jj, TURNS + 2 * i + jj // 2,
                                                  jj, 0 if jj % 2 else 4)
                                n = SLOTS3 * i + s
                                act.wait_ge(window_ready, WINDOWS + BATCHES2 + n + 1)
                                number_rows(n + 3, s % 3)

                    def body(k, p):
                        for u in range(2):
                            act.wait_ge(window_free, p * NB + 2 * k + u + (loop + slow) * LOOP_BATCHES + 1)
                            number_rows(2 * k + u, u)
                    if slow:
                        for_batches(act, body)
                    if layer % 2:
                        norm = layer // 2
                        act.wait_ge(var_ready, norms_before(slow, norm) + 1)
                        nc.scalar.activation(std[:, :], mv[:, :, 1], ACT.Sqrt, bias=eps[:, 0:1]).then_inc(std_ready, 1)

            act.wait_ge(mode_ready, 1)
            branch(act, rest_of)

        @block.tensor
        def _(pe):
            pe.wait_ge(ident_ready, 1)
            pe.wait_ge(edges_ready, 1)
            for c in range(CH):
                for a in range(EDGE_ARRAYS):
                    last = nc.tensor.transpose(ps[:, c, a * NB:(a + 1) * NB], edge_f[:, a, c * P:(c + 1) * P], ident[0:NB, 0:NB])
                last.then_inc(edges_turned, 1)
            pe.wait_ge(edges_copied, CH)
            pe.wait_ge(started_ready, 1)
            for c in range(CH):
                last = nc.tensor.matmul(ps[0:1, STARTS_BANK, 0:STRIPS], ones[0:NB, 0:1], started[:, c, :], start=(c == 0), stop=(c == CH - 1))
            last.then_inc(sums_ready, 1)
            pe.wait_ge(started_ready, 2)
            for c in range(CH):
                last = nc.tensor.matmul(ps[0:1, RSTARTS_BANK, 0:RSTRIPS + 1], ones[0:NB, 0:1], rstarted[:, c, :], start=(c == 0), stop=(c == CH - 1))
            last.then_inc(sums_ready, 1)
            nc.tensor.matmul(ps[0:1, SUMS_BANK, 0:NB], edge_f[:, DST, 0:1], ident[0:NB, 0:NB], start=True, stop=True)
            nc.tensor.matmul(ps[0:1, SUMS_BANK, NB:2 * NB], edge_f[:, DST, BATCH - 1:BATCH], ident[0:NB, 0:NB], start=True, stop=True)
            pe.wait_ge(inside_ready, 1)
            nc.tensor.matmul(ps[0:1, SUMS_BANK, 2 * NB:2 * NB + 2], ones[0:NB, 0:1], row_sums[:, :], start=True, stop=True).then_inc(sums_ready, 1)
            def count_strips(b, k):
                for u in range(2):
                    strip = b * (BANK // STRIP) + 2 * k + u
                    pe.wait_ge(strip_copied, strip + 1)
                    pe.wait_ge(hots_ready, strip + 3)
                    pe.wait_ge(lows_ready, strip + 3)
                    for c in range(STRIP_CH):
                        last = nc.tensor.matmul(ps[:, u, 0:CELLS], low_hot[:, u, c, :], cell_hot[:, u, c, :],
                                                start=(c == 0), stop=(c == STRIP_CH - 1))
                    last.then_inc(strip_counted, 1)

            def sum_degrees(b, tiles):
                if tiles[0] == 0:
                    pe.wait_ge(strip_copied, 2 + min(STRIPS, (b + 1) * BANK // STRIP))
                    if b >= 2:
                        pe.wait_ge(degrees_read, b - 1)
                for t in tiles:
                    last = nc.tensor.matmul(ps[:, DEG_BANK + b % 2, 0:block_width(b)], ones_h[:, :], block_of(b)[:, t, :],
                                            start=(t == 0), stop=(t == TILES - 1))
                if t == TILES - 1:
                    last.then_inc(degrees_ready, 1)

            def turn_degrees(b):
                pe.wait_ge(degrees_read, b + 1)
                for t in node_tiles(b):
                    last = nc.tensor.matmul(ps[:, CTX_BANK, 2 + t:3 + t], tin[0:1, t * P:(t + 1) * P], ones[0:1, 0:1],
                                            start=True, stop=True)
                return last

            pe.wait_ge(sums_read, 1)
            for b in range(NBLK):
                pairs = block_width(b) // STRIP // 2
                cuts = [1 + (pairs - 1) * c // SHARES for c in range(SHARES + 1)]
                count_strips(b, 0)
                for c in range(SHARES):
                    if b:
                        sum_degrees(b - 1, range(TILES * c // SHARES, TILES * (c + 1) // SHARES))
                    if cuts[c + 1] > cuts[c]:
                        with pe.Fori(cuts[c], cuts[c + 1]) as k:
                            count_strips(b, k)
                if b >= 2:
                    turn_degrees(b - 2)
            sum_degrees(NBLK - 1, range(TILES))
            pe.wait_ge(weights_loaded, 16 * W_LOADS)
            nc.tensor.matmul(ps[:, CTX_BANK, 0:1], wgate[:, :], ctx_c[:, :], start=True, stop=True)
            nc.tensor.matmul(ps[:, CTX_BANK, 1:2], wbias[:, :], ctx_c[:, :], start=True, stop=True)
            turn_degrees(NBLK - 2)
            turn_degrees(NBLK - 1).then_inc(gate_product, 1)
            pe.wait_ge(x_loaded, 32)
            for t in range(TILES):
                last = nc.tensor.transpose(ps[:, t // 4, (t % 4) * P:(t % 4 + 1) * P], xn[:, t, :], ident[:, :])
                if t % 4 == 3 or t == TILES - 1:
                    last.then_inc(x_turned, 1)
            pe.wait_ge(shift_ready, 1)

            def rest_of(slow):
                plan = products(slow)

                msgs, onehot = msgs_of(slow), onehot_of(slow)

                def window(u, left):
                    for j in range(CH):
                        last = nc.tensor.matmul(ps[:, WIN_BANK + u, 0:W], left(j), onehot[:, u, j, :], start=(j == 0), stop=(j == CH - 1))
                    last.then_inc(window_ready, 1)

                def windows(loop, gathers):
                    def body(k, p):
                        for u in range(2):
                            n = p * NB + 2 * k + u + loop * LOOP_BATCHES
                            pe.wait_ge(window_free, n + 1)
                            pe.wait_ge(onehot_ready, n + 1)
                            if gathers is not None:
                                pe.wait_ge(passes_done, gathers * PASSES + p + 1)
                                pe.wait_ge(gathered[u], (k + 1) * 16 * CH)
                            window(u, lambda j: ones[:, :] if gathers is None else msgs[u][:, j, :])
                    for_batches(pe, body)

                def sum_sources(layer, i, s, q, used):
                    for j, k in quarter(layer, s, q):
                        m = used + j
                        bank = 0 if layer == 3 and j % 2 else 4
                        if k == 0:
                            pe.wait_ge(rel_copied, m + 1 if layer == 2 else m)
                            if layer == 2:
                                pe.wait_ge(strip_copied, 2 + STRIPS + MADE2 * HSTRIPS * i + HSTRIPS * (j + 1))
                            else:
                                pe.wait_ge(halves_loaded[j], 16 * i + 16)
                        t, c = k // PARTS, k % PARTS
                        last = nc.tensor.matmul(ps[:, bank, 0:HCOLS], parts[:, c, t, :], halves[:, j, t * HCOLS:(t + 1) * HCOLS],
                                                start=(k == 0), stop=(k == TILES * PARTS - 1))
                        if k == TILES * PARTS - 1:
                            last.then_inc(rel_summed, 1)

                def slot_tail(layer, i, s, n, used, pairs_used, weights):
                    pe.wait_ge(window_free, n + (2 if layer == 2 else 3))
                    pe.wait_ge(onehot_ready, n + 1)
                    if layer == 2:
                        pe.wait_ge(gathered[s % 4], (2 * i + s // 4 + 1) * 16 * CH)
                        window(s % 2, lambda j: msgs[s % 4][:, j, :])
                    else:
                        pe.wait_ge(gathered[s % 3], (BATCHES2 // 4 + 2 * i + s // 3 + 1) * 16 * CH)
                        window(s % 2, lambda j: msgs[s % 3][:, j, :])
                    for j, a, b in use_of(layer, s):
                        if b == TILES * PARTS and j % 2:
                            pe.wait_ge(rel_copied, used + j + 2)
                            pe.wait_ge(rel_added, pairs_used + j // 2 + 1)
                            for r in range(R):
                                last = nc.tensor.matmul(ps[:, 5, 0:2 * HALF], weights[:, r, :], relsum[:, :, r * HALF:(r + 1) * HALF],
                                                        start=(r == 0), stop=(r == R - 1))
                            last.then_inc(rel_out, 1)

                def turn_y(g, bank):
                    for t in node_tiles(g):
                        last = nc.tensor.transpose(ps[:, bank, (t % 4) * P:(t % 4 + 1) * P], acc[:, t * P:(t + 1) * P], ident[:, :])
                    last.then_inc(y_turned, 1)

                def turn_back(g, bank):
                    pe.wait_ge(normed, node_tiles(g)[-1] + 1)
                    for t in node_tiles(g):
                        last = nc.tensor.transpose(ps[:, bank, (t % 4) * P:(t % 4 + 1) * P], xn[:, t, :], ident[:, :])
                    last.then_inc(xn_turned, 1)

                def turn_y_early(g):
                    if g >= 2:
                        pe.wait_ge(xT_copied, g - 1)
                    pe.wait_ge(block_read, NBLK + g + 1)
                    turn_y(g, WIN_BANK + g % 2)

                if slow:
                    windows(0, None)
                else:
                    for g in range(XG):
                        pe.wait_ge(diag_ready, g + 1)
                        nc.tensor.matmul(ps[:, g, 0:block_width(g)], ones[:, :], acc[:, g * BANK:g * BANK + block_width(g)],
                                         start=True, stop=True).then_inc(dinv_spread, 1)
                    pe.wait_ge(dinv_copied, XG)
                    for layer in range(2):
                        if layer:
                            pe.wait_ge(tin_ready, layer + 1)
                        for g in range(XG):
                            i = layer * XG + g
                            if not layer:
                                pe.wait_ge(scaled, g + 1)
                            if i >= 4:
                                pe.wait_ge(rest_ready, i - 3 if g >= 4 else layer * XG)
                            for t in node_tiles(g):
                                last = nc.tensor.matmul(ps[:, g % 4, (t % 4) * D:(t % 4 + 1) * D], tin[:, t * P:(t + 1) * P],
                                                        layer_w[layer][:, :], start=True, stop=True)
                            last.then_inc(feat_done, 1)
                        for b in range(NBLK):
                            i, n = layer * NBLK + b, block_width(b)
                            total = ps[:, DEG_BANK + i % 2, 0:n]
                            if i >= 2:
                                pe.wait_ge(block_read, i - 1)
                            nc.tensor.matmul(total, layer_self[layer][:, :], tin[:, b * BANK:b * BANK + n], start=True, stop=False)
                            pe.wait_ge(counts_loaded[i % 2], 16 * (i // 2 + 1))
                            for t in range(TILES):
                                if b == 0 and t % 4 == 0:
                                    pe.wait_ge(low_ready, layer * XG + t // 4 + 1)
                                for c in range(PARTS):
                                    last = nc.tensor.matmul(total, parts[:, c, t, :],
                                                            blocks[:, i % 2, t * n:(t + 1) * n],
                                                            start=False, stop=(t == TILES - 1 and c == PARTS - 1))
                            last.then_inc(block_summed, 1)
                            if layer and b:
                                turn_y_early(b - 1)
                            if layer and b >= 2:
                                turn_back(b - 2, WIN_BANK + b % 2)
                for loop, layer in enumerate(gather_layers(slow)):
                    left = layer_in[layer]
                    if slow or layer == 3:
                        pe.wait_ge(tin_ready, layer + 1)
                    else:
                        pe.wait_ge(block_read, 2 * NBLK)
                    if layer == 3 and not slow:
                        pe.wait_ge(strip_copied, 2 + STRIPS + RSTRIPS)
                    for g, kind, k, q in plan[layer]:
                        if layer == 3 and not slow and g % 3 == plan[layer][0][0] % 3 and (g - plan[layer][0][0]) // 3 < XG:
                            group = (g - plan[layer][0][0]) // 3
                            if group >= 2:
                                pe.wait_ge(rest_ready, 3 * XG + group - 1)
                            for t in node_tiles(group):
                                last = nc.tensor.transpose(ps[:, WIN_BANK + group % 2, (t % 4) * P:(t % 4 + 1) * P],
                                                           tin[:, t * P:(t + 1) * P], ident[:, :])
                            last.then_inc(feat_done, 1)
                        if g - TBANKS >= plan[layer][0][0]:
                            pe.wait_ge(*evacuated(g - TBANKS))
                        bank = g % TBANKS
                        if layer == 2 and not slow:
                            if g == NORM_AT[0]:
                                turn_y_early(XG - 1)
                            elif g == NORM_AT[1]:
                                turn_back(XG - 2, WIN_BANK + XG % 2)
                            elif g == NORM_AT[2]:
                                turn_back(XG - 1, WIN_BANK + (XG - 1) % 2)
                            pe.wait_ge(xT_copied, (k // 2 // 4 if kind == "table" else XG - 1) + 1)
                        if kind == "self":
                            n = block_width(k)
                            last = nc.tensor.matmul(ps[:, bank, 0:n], layer_self[layer][:, :], left[:, k * BANK:k * BANK + n],
                                                    start=True, stop=True)
                        elif layer < 2:
                            for t in node_tiles(k):
                                last = nc.tensor.matmul(ps[:, bank, (t % 4) * D:(t % 4 + 1) * D], left[:, t * P:(t + 1) * P],
                                                        layer_w[layer][:, :], start=True, stop=True)
                        else:
                            t, h = k // 2, k % 2
                            last = nc.tensor.matmul(ps[:, bank, :], left[:, t * P:(t + 1) * P],
                                                    layer_w[layer][:, 4 * h:4 * h + 4, :].rearrange("p r f -> p (r f)"),
                                                    start=True, stop=True)
                        last.then_inc(product_done, 1)
                    if slow:
                        windows(loop + slow, loop)
                    elif layer == 2:
                        for g in (plan[layer][-2][0], plan[layer][-1][0]):
                            pe.wait_ge(*evacuated(g))
                        with pe.Fori(0, TURNS) as i:
                            for s in range(SLOTS2):
                                for q in range(4):
                                    strip, u = STRIPS + MADE2 * HSTRIPS * i + 4 * s + q, q % 2
                                    pe.wait_ge(strip_copied, strip + 1)
                                    pe.wait_ge(hots_ready, strip + 3)
                                    pe.wait_ge(lows_ready, strip + 3)
                                    for c in range(RSTRIP_CH):
                                        for h in range(2):
                                            last = nc.tensor.matmul(ps[:, 2 * u + h, 0:CELLS], low_hot[:, u, c, :],
                                                                    rcell_hot[:, u, c, h * CELLS:(h + 1) * CELLS],
                                                                    start=(c == 0), stop=(c == RSTRIP_CH - 1))
                                    last.then_inc(strip_counted, 1)
                                    sum_sources(2, i, s, q, USED2 * i)
                                slot_tail(2, i, s, SLOTS2 * i + s, USED2 * i, i, wr1)
                    else:
                        for g in (plan[layer][-2][0], plan[layer][-1][0]):
                            pe.wait_ge(*evacuated(g))
                        with pe.Fori(0, TURNS) as i:
                            for s in range(SLOTS3):
                                for q in range(4):
                                    sum_sources(3, i, s, q, TURNS * USED2 + USED3 * i)
                                slot_tail(3, i, s, BATCHES2 + SLOTS3 * i + s, TURNS * USED2 + USED3 * i,
                                          TURNS + 2 * i, wr2)
                    if layer % 2:
                        pe.wait_ge(y_ready, layer // 2 + 1)
                        for g in range(XG):
                            turn_y(g, g)
                        if layer == 1:
                            for g in range(XG):
                                turn_back(g, g)

            pe.wait_ge(mode_ready, 1)
            branch(pe, rest_of)

        @block.vector
        def _(dve):
            steps = [0]

            def then(ins):
                steps[0] += 1
                ins.then_inc(dve_step, 1)
                dve.wait_ge(dve_step, steps[0])

            nc.vector.memset(xn[:, TILES - 1, :], 0.0).then_inc(x_cleared, 1)
            nc.vector.memset(ones[:, :], 1.0)
            nc.vector.memset(ones_h[:, :], 1.0)
            nc.vector.memset(eps[:, :], LN_EPS)
            dve.sem_inc(window_free, 2)
            dve.sem_inc(lows_ready, 2)
            dve.sem_inc(hots_ready, 2)
            dve.sem_inc(window_ready, WINDOWS)
            dve.sem_inc(rel_summed, SUMMED)
            dve.sem_inc(rel_copied, 1)
            dve.sem_inc(rel_out, 1)
            dve.sem_inc(rel_added, 1)
            dve.sem_inc(passes_done, 1)
            for j in range(MADE2):
                dve.sem_inc(halves_stored[j], 16)
            dve.sem_inc(strip_counted, 2)
            dve.sem_inc(strip_copied, 2)
            dve.wait_ge(edges_loaded, EDGE_LOADS * 16)
            f = [edge_f[:, a, :] for a in range(EDGE_ARRAYS)]
            then(nc.vector.tensor_scalar(f[KEY].bitcast(i32), src_i, 7, None, ALU.logical_shift_right))
            then(nc.vector.tensor_copy(f[LOW], f[KEY].bitcast(i32)))
            nc.vector.tensor_copy(f[DST], dst_i)
            nc.vector.tensor_copy(f[RKEY], src_i)
            then(nc.vector.tensor_copy(f[ROW], rel_i))
            nc.vector.scalar_tensor_tensor(out=f[KEY], in0=f[DST], scalar=float(-TILES), in1=f[LOW], op0=ALU.mult, op1=ALU.subtract)
            then(nc.vector.scalar_tensor_tensor(out=inside, in0=f[ROW], scalar=float(-TILES), in1=f[LOW], op0=ALU.mult, op1=ALU.subtract))
            nc.vector.scalar_tensor_tensor(out=f[ROW], in0=f[RKEY], scalar=float(R), in1=f[ROW], op0=ALU.mult, op1=ALU.add)
            then(nc.vector.scalar_tensor_tensor(out=f[LOW], in0=f[LOW], scalar=float(P), in1=f[RKEY], op0=ALU.mult, op1=ALU.subtract))
            then(nc.vector.scalar_tensor_tensor(out=f[RKEY], in0=f[DST], scalar=float(-RKEYS), in1=inside, op0=ALU.mult, op1=ALU.add))
            dve.sem_inc(edges_ready, 1)
            for c in range(CH):
                dve.wait_ge(edges_turned, c + 1)
                nc.vector.tensor_copy(edges[:, :, :, c], ps[:, c, 0:EDGE_ARRAYS * NB].rearrange("p (a b) -> p a b", a=EDGE_ARRAYS))\
                    .then_inc(edges_copied, 1)
            dve.wait_ge(patterns_ready, 6)
            for c in range(CH):
                last = nc.vector.tensor_scalar(started[:, c, :], strip_node[0:NB, :], f[DST][:, c * P:c * P + 1], None, ALU.is_gt)
            last.then_inc(started_ready, 1)
            for c in range(CH):
                last = nc.vector.tensor_scalar(rstarted[:, c, :], rstrip_node[0:NB, :], f[DST][:, c * P:c * P + 1], None, ALU.is_gt)
            last.then_inc(started_ready, 1)
            dve.wait_ge(sums_ready, 1)
            then(nc.vector.tensor_scalar(start_f[:, :], ps[0:1, STARTS_BANK, 0:STRIPS], -1.0, 0.0, ALU.add, ALU.max))
            nc.vector.memset(start_i[:, STRIPS:STRIPS + 2], 0)
            nc.vector.tensor_scalar(start_i[:, 0:STRIPS], start_f[:, :], float(NB * CH - STRIP_CH), None, ALU.min).then_inc(starts_ready, 1)
            then(nc.vector.tensor_scalar(inside, f[DST], f[DST][:, 0:1], None, ALU.subtract))
            then(nc.vector.tensor_scalar(nonneg, inside, 0.0, None, ALU.is_ge))
            then(nc.vector.scalar_tensor_tensor(out=inside, in0=inside, scalar=float(W), in1=nonneg, op0=ALU.is_lt, op1=ALU.mult))
            then(nc.vector.reduce_sum(row_sums[:, 0:1], inside, AX.X))
            then(nc.vector.tensor_tensor(inside[:, 0:BATCH - 1], f[DST][:, 1:BATCH], f[DST][:, 0:BATCH - 1], ALU.is_lt))
            nc.vector.reduce_sum(row_sums[:, 1:2], inside[:, 0:BATCH - 1], AX.X).then_inc(inside_ready, 1)
            dve.wait_ge(sums_ready, 2)
            then(nc.vector.tensor_scalar(rstart_f[:, :], ps[0:1, RSTARTS_BANK, 0:RSTRIPS], -1.0, 0.0, ALU.add, ALU.max))
            then(nc.vector.tensor_scalar(rstart_f[:, :], rstart_f[:, :], float(NB * CH - RSTRIP_CH), None, ALU.min))
            nc.vector.tensor_copy(rstart_i[:, :], rstart_f[:, :])
            nc.vector.scalar_tensor_tensor(out=faults[:, 0:RSTRIPS], in0=rstart_f[:, :], scalar=float(RSTRIP_CH),
                                           in1=ps[0:1, RSTARTS_BANK, 1:RSTRIPS + 1], op0=ALU.add, op1=ALU.is_lt)
            dve.wait_ge(sums_ready, 3)
            nc.vector.memset(base_i[:, 0:1], NP)
            nc.vector.tensor_copy(base_i[:, 1:1 + NB], ps[0:1, SUMS_BANK, 0:NB])
            then(nc.vector.tensor_copy(firsts[:, :], ps[0:1, SUMS_BANK, 0:NB]))
            nc.vector.tensor_tensor(faults[:, RSTRIPS:RSTRIPS + NB - 1], firsts[:, 1:NB], ps[0:1, SUMS_BANK, NB:2 * NB - 1], ALU.is_lt)
            for c, (batches, split) in enumerate(((BATCHES2, SPLIT2), (BATCHES3, SPLIT3))):
                at = RSTRIPS + NB - 1 + c
                nc.vector.tensor_scalar(faults[:, at:at + 1], firsts[:, batches:batches + 1], float(split), None, ALU.is_lt)
            then(nc.vector.tensor_copy(sums[:, 2:4], ps[0:1, SUMS_BANK, 2 * NB:2 * NB + 2]))
            dve.sem_inc(sums_read, 1)
            then(nc.vector.reduce_sum(sums[:, 0:1], faults[:, :], AX.X))
            then(nc.vector.tensor_tensor(sums[:, 3:4], sums[:, 3:4], sums[:, 0:1], ALU.add))
            then(nc.vector.tensor_scalar(sums[:, 3:4], sums[:, 3:4], 0.0, None, ALU.is_equal))
            then(nc.vector.tensor_tensor(sums[:, 0:1], sums[:, 2:3], sums[:, 3:4], ALU.mult))
            dve.wait_ge(edges_copied, CH)
            dve.wait_ge(starts_ready, 1)

            def make_strip_keys(strip, place, start):
                nc.vector.tensor_scalar(strip_keys[:, place, :], chunk_of[KEY][:, bass.ds(start, STRIP_CH)],
                                        strip_key[:, bass.ds(strip, 1)], None, ALU.add).then_inc(keys_ready, 1)

            def strip_hots(strip, u, keys, start):
                dve.wait_ge(keys_ready, strip + 1)
                dve.wait_ge(strip_counted, strip + 1)
                for c in range(DVE_LOWS):
                    nc.vector.tensor_scalar(low_hot[:, u, c, :], cell_h[:, 0:P], chunk_of[LOW][:, bass.ds(start + c, 1)],
                                            0.0, ALU.add, ALU.is_equal)
                for c in range(STRIP_CH):
                    last = nc.vector.tensor_scalar(cell_hot[:, u, c, :], cell_h[:, 0:CELLS], keys[:, c:c + 1],
                                                   0.0, ALU.add, ALU.is_equal)
                last.then_inc(hots_ready, 1)

            def read_degrees(b):
                dve.wait_ge(degrees_ready, b + 1)
                nc.vector.tensor_scalar(tin[:, b * BANK:b * BANK + block_width(b)], ps[:, DEG_BANK + b % 2, 0:block_width(b)],
                                        1.0, 1.0, ALU.add, ALU.max).then_inc(degrees_read, 1)

            quads = STRIPS // 4
            starts = load_row(dve, start_i, 0, 2, NB * CH - STRIP_CH)
            for u in range(2):
                make_strip_keys(u, u, starts[u])
            for b in range(NBLK):
                with dve.Fori(b * (BANK // STRIP // 4), min(quads, (b + 1) * (BANK // STRIP // 4))) as k:
                    starts = load_row(dve, start_i, 4 * k, 6, NB * CH - STRIP_CH)
                    for h in range(2):
                        for u in range(2):
                            dve.wait_ge(hots_ready, 4 * k + 2 * h + u + 1)
                            make_strip_keys(4 * k + 2 * h + u + 2, (2 * h + u + 2) % 4, starts[2 * h + u + 2])
                            strip_hots(4 * k + 2 * h + u, u, strip_keys[:, 2 * h + u, :], starts[2 * h + u])
                if b:
                    read_degrees(b - 1)
            read_degrees(NBLK - 1)
            dve.wait_ge(degrees_read, NBLK)
            then(nc.vector.reduce_sum(sums[:, 1:2], tin[0:1, :], AX.X))
            then(nc.vector.tensor_scalar(sums[:, 1:2], sums[:, 1:2], float(-NP), None, ALU.add))
            then(nc.vector.tensor_tensor(sums[:, 0:1], sums[:, 0:1], sums[:, 1:2], ALU.min))
            nc.vector.tensor_scalar(flag_i[:, :], sums[:, 0:1], float(E), None, ALU.is_equal).then_inc(mode_ready, 1)
            dve.wait_ge(degrees_sqrt, 1)
            dve.wait_ge(gate_ready, 1)
            nc.vector.scalar_tensor_tensor(out=shift[:, :], in0=cols[:, 1:2], scalar=gate[:, 0:1], in1=ps[:, CTX_BANK, 1:2],
                                           op0=ALU.mult, op1=ALU.add).then_inc(shift_ready, 1)
            dve.wait_ge(x_copied, XG)
            dve.wait_ge(mode_ready, 1)
            steps_before = steps[0]

            def rest_of(slow):
                steps[0] = steps_before
                plan = products(slow)
                onehot = onehot_of(slow)
                dst_t = edges[:, DST, :, :].rearrange("p b c -> p (b c)")
                then(nc.vector.tensor_scalar(dst_t, dst_t, 1.0, None, ALU.add))

                def make_onehot(batch, u, base):
                    nc.vector.tensor_tensor(
                        onehot[:, u, :, :],
                        edges[:, DST, bass.ds(batch, 1), :].rearrange("p a c -> p (a c)").unsqueeze(2).to_broadcast([P, CH, W]),
                        node_id[:, bass.ds(base, W)].unsqueeze(1).to_broadcast([P, CH, W]),
                        ALU.is_equal).then_inc(onehot_ready, 1)

                def add_window(layer, n, u, base, dense):
                    dve.wait_ge(window_ready, WINDOWS + n + 1)
                    dve.wait_ge(window_free, n + (3 if layer == 2 else 4))
                    dve.wait_ge(rel_added, dense + 1)
                    part = acc[:, bass.ds(base, W)]
                    nc.vector.tensor_tensor(part, part, ps[:, WIN_BANK + u, 0:W], ALU.add).then_inc(window_free, 1)

                def add_pair(layer, pair, n, number):
                    dve.wait_ge(rel_out, pair + 2)
                    dve.wait_ge(window_free, n + (4 if layer == 2 else 5))
                    dve.wait_ge(rel_added, pair + 1)
                    part = acc[:, bass.ds(SPLIT3 + HALF * number, 2 * HALF)]
                    nc.vector.tensor_tensor(part, part, ps[:, 5, 0:2 * HALF], ALU.add).then_inc(rel_added, 1)

                def mask(split):
                    then(nc.vector.scalar_tensor_tensor(out=dst_t, in0=dst_t, scalar=float(split + 1), in1=dst_t,
                                                        op0=ALU.is_lt, op1=ALU.mult))

                def split_step(layer, g):
                    if g < XG:
                        dve.wait_ge(high_ready, layer * XG + g + 1)
                        nc.vector.tensor_tensor(rest[:, g % 4, 0:block_width(g)], features(layer, g), parts_of(node_tiles(g))[0],
                                                ALU.subtract).then_inc(rest_ready, 1)
                    if g:
                        part = parts_of(node_tiles(g - 1))
                        dve.wait_ge(mid_ready, layer * XG + g)
                        nc.vector.tensor_tensor(part[2], rest[:, (g - 1) % 4, 0:block_width(g - 1)], part[1],
                                                ALU.subtract).then_inc(low_ready, 1)

                def windows(loop, total):
                    def body(k, p):
                        base = p * W
                        for u in range(2):
                            make_onehot(2 * k + u, u, base)
                        for u in range(2):
                            n = p * NB + 2 * k + u + loop * LOOP_BATCHES
                            dve.wait_ge(window_ready, WINDOWS + n + 1)
                            dve.wait_ge(window_free, n + 2)
                            part = total[:, bass.ds(base, W)]
                            nc.vector.tensor_tensor(part, part, ps[:, WIN_BANK + u, 0:W], ALU.add).then_inc(window_free, 1)
                    for_batches(dve, body)
                    dve.wait_ge(window_free, (loop + 1) * LOOP_BATCHES + 2)

                def layer_norm(norm):
                    for t in range(TILES):
                        dve.wait_ge(y_turned, norm * XG + t // 4 + 1)
                        last = nc.vector.bn_stats(stats[:, t, :], ps[:, t // 4, (t % 4) * P:(t % 4 + 1) * P])
                    then(last)
                    for t in range(TILES):
                        last = nc.vector.bn_aggr(mv[:, t, :], stats[:, t, :])
                    last.then_inc(var_ready, 1)
                    dve.wait_ge(std_ready, norms_before(slow, norm) + 1)
                    then(nc.vector.reciprocal(rstd[:, :], std[:, :]))
                    for t in range(TILES):
                        nc.vector.tensor_scalar(xn[:, t, :], ps[:, t // 4, (t % 4) * P:(t % 4 + 1) * P], mv[:, t, 0:1],
                                                rstd[:, t:t + 1], ALU.subtract, ALU.mult).then_inc(normed, 1)

                def copy_back(g, bank):
                    n = block_width(g)
                    dve.wait_ge(xn_turned, g + 1)
                    nc.vector.tensor_copy(xT[:, g * BANK:g * BANK + n], ps[:, bank, 0:n]).then_inc(xT_copied, 1)

                def norm_group(g):
                    bank, tiles = WIN_BANK + g % 2, slice(node_tiles(g)[0], node_tiles(g)[-1] + 1)
                    dve.wait_ge(y_turned, g + 1)
                    for t in node_tiles(g):
                        last = nc.vector.bn_stats(stats[:, t, :], ps[:, bank, (t % 4) * P:(t % 4 + 1) * P])
                    then(last)
                    for t in node_tiles(g):
                        last = nc.vector.bn_aggr(mv[:, t, :], stats[:, t, :])
                    last.then_inc(var_ready, 1)
                    dve.wait_ge(std_ready, g + 1)
                    then(nc.vector.reciprocal(rstd[:, tiles], std[:, tiles]))
                    for t in node_tiles(g):
                        nc.vector.tensor_scalar(xn[:, t, :], ps[:, bank, (t % 4) * P:(t % 4 + 1) * P], mv[:, t, 0:1],
                                                rstd[:, t:t + 1], ALU.subtract, ALU.mult).then_inc(normed, 1)

                def first_layer_end(sums_, cut):
                    then(nc.vector.tensor_tensor(acc[:, cut], sums_, dinv[:, cut], ALU.mult))
                    then(nc.vector.tensor_scalar(acc[:, cut], acc[:, cut], cols[:, 0:1], None, ALU.add))
                    then(nc.vector.scalar_tensor_tensor(out=acc[:, cut], in0=acc[:, cut], scalar=SLOPE, in1=acc[:, cut],
                                                        op0=ALU.mult, op1=ALU.max))
                    return nc.vector.tensor_tensor(tin[:, cut], acc[:, cut], dinv[:, cut], ALU.mult)

                def second_layer_end(sums_, cut):
                    then(nc.vector.tensor_tensor(acc[:, cut], sums_, dinv[:, cut], ALU.mult))
                    then(nc.vector.tensor_scalar(acc[:, cut], acc[:, cut], gate[:, 0:1], shift[:, 0:1], ALU.mult, ALU.add))
                    return nc.vector.tensor_tensor(acc[:, cut], acc[:, cut], xT[:, cut], ALU.add)

                everything = slice(0, NP)
                if slow:
                    blocks_stored(dve)
                    key_t, low_t = chunk_of[KEY], chunk_of[LOW]
                    then(nc.vector.tensor_scalar(key_t, key_t, float(-P), float(P * TILES), ALU.mult, ALU.add))
                    then(nc.vector.scalar_tensor_tensor(out=key_t, in0=dst_t, scalar=float(-P * TILES), in1=key_t, op0=ALU.mult, op1=ALU.add))
                    then(nc.vector.tensor_tensor(key_t, key_t, low_t, ALU.subtract))
                    then(nc.vector.memset(dinv[:, :], 1.0))
                    windows(0, dinv)
                    then(nc.vector.tensor_scalar(dinv[:, :], dinv[:, :], 1.0, None, ALU.max))
                    nc.vector.reciprocal(dinv[:, :], dinv[:, :]).then_inc(deg_ready, 1)
                    dve.wait_ge(deg_sqrt, 1)
                    nc.vector.tensor_tensor(tin[:, :], xT[:, :], dinv[:, :], ALU.mult).then_inc(tin_ready, 1)
                else:
                    then(nc.vector.reciprocal(dinv_col[:, :], dinv_col[:, :]))
                    for g in range(XG):
                        n = len(node_tiles(g))
                        nc.vector.tensor_tensor(acc[:, g * BANK:g * BANK + n * P].rearrange("p (t n) -> p t n", t=n),
                                                ident[:, :].unsqueeze(1).to_broadcast([P, n, P]),
                                                dinv_col[:, 4 * g:4 * g + n].unsqueeze(2).to_broadcast([P, n, P]),
                                                ALU.mult).then_inc(diag_ready, 1)
                    for g in range(XG):
                        cut = slice(g * BANK, g * BANK + block_width(g))
                        dve.wait_ge(dinv_copied, g + 1)
                        nc.vector.tensor_tensor(tin[:, cut], xT[:, cut], dinv[:, cut], ALU.mult).then_inc(scaled, 1)
                    dve.sem_inc(tin_ready, 1)
                if not slow:
                    for layer in range(2):
                        for g in range(XG + 1):
                            split_step(layer, g)
                        for b in range(NBLK):
                            i, n = layer * NBLK + b, block_width(b)
                            cut = slice(b * BANK, b * BANK + n)
                            dve.wait_ge(block_summed, i + 1)
                            end = (second_layer_end if layer else first_layer_end)(ps[:, DEG_BANK + i % 2, 0:n], cut)
                            end.then_inc(block_read, 1)
                            if layer and b:
                                norm_group(b - 1)
                            if layer and b >= 2:
                                copy_back(b - 2, WIN_BANK + b % 2)
                        dve.wait_ge(block_read, (layer + 1) * NBLK)
                        dve.sem_inc(y_ready if layer else tin_ready, 1)
                for loop, layer in enumerate(gather_layers(slow)):
                    if not slow:
                        mask(SPLIT2 if layer == 2 else SPLIT3)
                        if layer == 3:
                            for j in range(MADE2):
                                dve.wait_ge(halves_stored[j], 16 * (TURNS + 1))
                    for g, kind, k, q in plan[layer]:
                        if g % 2:
                            continue
                        if layer == 2 and not slow:
                            if g == NORM_AT[0] + 2:
                                norm_group(XG - 1)
                            elif g == NORM_AT[1] + 2:
                                copy_back(XG - 2, WIN_BANK + XG % 2)
                            elif g == NORM_AT[2] + 2:
                                copy_back(XG - 1, WIN_BANK + (XG - 1) % 2)
                                dve.sem_inc(tin_ready, 1)
                        if not slow:
                            for step in split_steps_at(g - plan[layer][0][0]):
                                split_step(layer, step)
                        dve.wait_ge(product_done, g + 1)
                        if kind == "table":
                            n = table_view(layer, k)[1]
                            if q >= STAGES:
                                dve.wait_ge(stored[q % STAGES], 16 * (q // STAGES))
                            nc.vector.tensor_copy(stage[:, q % STAGES, 0:n], ps[:, g % TBANKS, 0:n]).then_inc(dve_evac, 1)
                        else:
                            n = block_width(k)
                            own = acc[:, k * BANK:k * BANK + n]
                            if layer < 2:
                                nc.vector.tensor_copy(own, ps[:, g % TBANKS, 0:n]).then_inc(dve_evac, 1)
                            else:
                                nc.vector.tensor_scalar(own, ps[:, g % TBANKS, 0:n], cols[:, 1 + layer:2 + layer], None,
                                                        ALU.add).then_inc(dve_evac, 1)
                    for g in (plan[layer][-2][0], plan[layer][-1][0]):
                        dve.wait_ge(*evacuated(g))
                    if slow:
                        windows(loop + slow, acc)
                    else:
                        then(nc.vector.memset(acc[:, NP:NP + W], 0.0))
                        if layer == 2:
                            then(nc.vector.memset(ps[:, WIN_BANK + 1, 0:W], 0.0))
                        slots = SLOTS2 if layer == 2 else SLOTS3
                        first_n = 0 if layer == 2 else BATCHES2
                        with dve.Fori(0, TURNS) as i:
                            for s in range(slots):
                                batch = slots * i + s
                                before_base, base = load_row(dve, base_i, batch, 2, NP)
                                make_onehot(batch, s % 2, base)
                                if layer == 2:
                                    local = MADE2 * HSTRIPS * i + 4 * s
                                    where = half_number(i, s // 2) * HSTRIPS + 4 * (s % 2)
                                    starts = load_row(dve, rstart_i, where, 4, NB * CH - RSTRIP_CH)
                                    dve.wait_ge(hots_ready, STRIPS + local + 2)
                                    for q in range(4):
                                        nc.vector.tensor_scalar(strip_keys[:, q, 0:RSTRIP_CH], chunk_of[RKEY][:, bass.ds(starts[q], RSTRIP_CH)],
                                                                rstrip_key[:, bass.ds(where + q, 1)], None, ALU.add).then_inc(keys_ready, 1)
                                    for q in range(4):
                                        strip, u = STRIPS + local + q, q % 2
                                        dve.wait_ge(keys_ready, strip + 3)
                                        dve.wait_ge(strip_counted, strip + 1)
                                        for c in range(RSTRIP_CH - 1):
                                            nc.vector.tensor_scalar(low_hot[:, u, c, :], cell_h[:, 0:P], chunk_of[LOW][:, bass.ds(starts[q] + c, 1)],
                                                                    0.0, ALU.add, ALU.is_equal)
                                        for c in range(RSTRIP_CH):
                                            last = nc.vector.tensor_scalar(rcell_hot[:, u, c, :], cell_h[:, :], strip_keys[:, q, c:c + 1],
                                                                           0.0, ALU.add, ALU.is_equal)
                                        last.then_inc(hots_ready, 1)
                                pairs_before = i if layer == 2 else TURNS + 2 * i
                                done = [j for t in range(s - 1) for j in pairs_of(layer, t)]
                                add_window(layer, first_n + batch - 1, (s - 1) % 2, before_base, pairs_before + len(done))
                                for t in ((s - 1,) if s < slots - 1 else (s - 1, s)):
                                    for j in pairs_of(layer, t) if t >= 0 else []:
                                        add_pair(layer, pairs_before + j // 2, first_n + batch - 1,
                                                 half_number(i, 0) if layer == 2 else USED3 * i + j - 1)
                        (final_base,) = load_row(dve, base_i, slots * TURNS, 1, NP)
                        add_window(layer, first_n + slots * TURNS - 1, 1, final_base, TURNS * (1 if layer == 2 else 3))
                        dve.wait_ge(window_free, first_n + slots * TURNS - 1 + (4 if layer == 2 else 5))
                    if layer == 0:
                        first_layer_end(acc[:, 0:NP], everything).then_inc(tin_ready, 1)
                    elif layer == 1:
                        second_layer_end(acc[:, 0:NP], everything).then_inc(y_ready, 1)
                        layer_norm(0)
                        for g in range(XG):
                            copy_back(g, g)
                        dve.wait_ge(xT_copied, XG)
                        dve.sem_inc(tin_ready, 1)
                    elif layer == 2:
                        nc.vector.tensor_scalar(tin[:, :], acc[:, 0:NP], 0.0, None, ALU.max).then_inc(tin_ready, 1)
                    else:
                        nc.vector.scalar_tensor_tensor(out=acc[:, 0:NP], in0=acc[:, 0:NP], scalar=0.0, in1=xT[:, :],
                                                       op0=ALU.max, op1=ALU.add).then_inc(y_ready, 1)
                        layer_norm(1)

            branch(dve, rest_of)


_INS = ['x', 'src', 'dst', 'edge_type_8', 'L0_gnn_ctx', 'L0_gnn_W1', 'L0_gnn_b1', 'L0_gnn_W2', 'L0_gnn_b2', 'L0_gnn_Wg',
        'L0_gnn_bg', 'L0_gnn_Wb', 'L1_gnn_w1', 'L1_gnn_sl1', 'L1_gnn_b1', 'L1_gnn_w2', 'L1_gnn_sl2', 'L1_gnn_b2']


def kernel(**inputs):
    import numpy as _np
    import concourse.bacc as _bacc
    from concourse import mybir as _mybir
    from concourse.bass_utils import run_bass_kernel_spmd as _run

    nc = _bacc.Bacc("TRN2", target_bir_lowering=False, num_devices=1)
    arrays, args = {}, {}
    for name in _INS:
        a = _np.ascontiguousarray(inputs[name])
        arrays[f"in_{name}"] = a
        args[name] = nc.dram_tensor(f"in_{name}", a.shape, _mybir.dt.from_np(a.dtype), kind="ExternalInput").ap()
    out = nc.dram_tensor("out_0", (N_NODES, D), _mybir.dt.float32, kind="ExternalOutput").ap()
    gnn_kernel(nc, *[args[n] for n in _INS], out)
    r = _run(nc, [arrays], core_ids=[0])
    return r.results[0]["out_0"]
```
